# Optimizing a Trainium2 kernel written in Bass

```python
import numpy as np
import jax
import jax.numpy as jnp

def _softmax(x, axis=-1):
    return jax.nn.softmax(x, axis=axis)

def _gelu(x):
    return jax.nn.gelu(x, approximate=True)

def _silu(x):
    return jax.nn.silu(x)

def _sigmoid(x):
    return jax.nn.sigmoid(x)

def _layernorm(x, axis=-1, eps=1e-05):
    m = jnp.mean(x, axis=axis, keepdims=True)
    v = jnp.var(x, axis=axis, keepdims=True)
    return (x - m) / jnp.sqrt(v + eps)

def _scatter_add(tgt, idx, src, axis=0):
    return tgt.at[idx].add(src)

def _segment_sum(src, seg, n):
    return jax.ops.segment_sum(src, seg, n)
kernel_name = 'mk_lm_tower_d1_tok_ids1024_r4_e93758'

def setup_inputs(seed: int=0):
    np.random.seed(seed)
    _w = jnp.asarray

    def _rec_inputs():
        import jax
        import jax.numpy as jnp
        _rk = jax.random.key(seed)
        x = jax.random.randint(jax.random.fold_in(_rk, 1), (16, 1024), 0, 12564, jnp.int32)
        return x
    x = _rec_inputs()

    def _L0_tok_setup():
        import jax, jax.numpy as jnp
        import numpy as np
        VOCAB = 50257
        NUM_DIM = 256
        BATCH = 4
        SEQ = 1024
        key = jax.random.key(seed)
        k_tok, k_w, k_b = jax.random.split(key, 3)
        tokens = jax.random.randint(k_tok, (BATCH, SEQ), 0, VOCAB)
        weight = jax.random.normal(k_w, (NUM_DIM, VOCAB), dtype=jnp.float32) * 0.02
        bias = jax.random.normal(k_b, (NUM_DIM,), dtype=jnp.float32) * 0.02
        return {'tokens': tokens, 'weight': weight, 'bias': bias}
    _L0_tok_all = _L0_tok_setup()
    _L0_tok_in = {k: v for k, v in _L0_tok_all.items() if k in ('weight', 'bias')}
    del _L0_tok_all

    def _L0_attn_setup():
        import jax, jax.numpy as jnp
        import numpy as np
        EMBED_DIM = 256
        NUM_HEADS = 16
        HEAD_DIM = EMBED_DIM // NUM_HEADS
        SCALE = HEAD_DIM ** (-0.5)
        key = jax.random.key(seed)
        ks = jax.random.split(key, 5)
        B, N, C = (2, 512, EMBED_DIM)
        x = jax.random.normal(ks[0], (B, N, C), dtype=jnp.float32)
        w_qkv = jax.random.normal(ks[1], (3 * C, C), dtype=jnp.float32) * C ** (-0.5)
        b_qkv = jax.random.normal(ks[2], (3 * C,), dtype=jnp.float32) * 0.01
        w_out = jax.random.normal(ks[3], (C, C), dtype=jnp.float32) * C ** (-0.5)
        b_out = jax.random.normal(ks[4], (C,), dtype=jnp.float32) * 0.01
        return {'x': x, 'w_qkv': w_qkv, 'b_qkv': b_qkv, 'w_out': w_out, 'b_out': b_out}
    _L0_attn_all = _L0_attn_setup()
    _L0_attn_in = {k: v for k, v in _L0_attn_all.items() if k in ('w_qkv', 'b_qkv', 'w_out', 'b_out')}
    del _L0_attn_all

    def _L0_ffn_setup():
        import jax, jax.numpy as jnp
        import numpy as np
        D_MODEL = 256
        D_FF = 512
        NUM_EXPERTS = 16
        TOP_K = 2
        CAPACITY_FACTOR = 1.25
        BATCH, SEQ = (4, 512)
        key = jax.random.key(seed)
        k0, k1, k2, k3 = jax.random.split(key, 4)
        x = jax.random.normal(k0, (BATCH, SEQ, D_MODEL), jnp.float32)
        gate_w = jax.random.normal(k1, (NUM_EXPERTS, D_MODEL), jnp.float32) / np.float32(np.sqrt(D_MODEL))
        w1 = jax.random.normal(k2, (NUM_EXPERTS, D_MODEL, D_FF), jnp.float32) / np.float32(np.sqrt(D_MODEL))
        w2 = jax.random.normal(k3, (NUM_EXPERTS, D_FF, D_MODEL), jnp.float32) / np.float32(np.sqrt(D_FF))
        return {'x': x, 'gate_w': gate_w, 'w1': w1, 'w2': w2}
    _L0_ffn_all = _L0_ffn_setup()
    _L0_ffn_in = {k: v for k, v in _L0_ffn_all.items() if k in ('gate_w', 'w1', 'w2')}
    del _L0_ffn_all
    return {'x': x, 'L0_tok_weight': _L0_tok_in['weight'], 'L0_tok_bias': _L0_tok_in['bias'], 'L0_attn_w_qkv': _L0_attn_in['w_qkv'], 'L0_attn_b_qkv': _L0_attn_in['b_qkv'], 'L0_attn_w_out': _L0_attn_in['w_out'], 'L0_attn_b_out': _L0_attn_in['b_out'], 'L0_ffn_gate_w': _L0_ffn_in['gate_w'], 'L0_ffn_w1': _L0_ffn_in['w1'], 'L0_ffn_w2': _L0_ffn_in['w2']}

def reference(x, L0_tok_weight, L0_tok_bias, L0_attn_w_qkv, L0_attn_b_qkv, L0_attn_w_out, L0_attn_b_out, L0_ffn_gate_w, L0_ffn_w1, L0_ffn_w2):
    import jax
    import jax.numpy as jnp

    def _L0_tok_ref(tokens, weight, bias):
        import jax, jax.numpy as jnp
        import numpy as np
        VOCAB = 50257
        NUM_DIM = 256
        BATCH = 4
        SEQ = 1024
        table = weight.T
        return jnp.take(table, tokens, axis=0) + bias

    def _L0_attn_ref(x, w_qkv, b_qkv, w_out, b_out):
        import jax, jax.numpy as jnp
        import numpy as np
        EMBED_DIM = 256
        NUM_HEADS = 16
        HEAD_DIM = EMBED_DIM // NUM_HEADS
        SCALE = HEAD_DIM ** (-0.5)
        B, N, C = x.shape
        H, D = (NUM_HEADS, HEAD_DIM)
        qkv = x @ w_qkv.T + b_qkv
        qkv = qkv.reshape(B, N, 3, H, D)
        q = qkv[:, :, 0].transpose(0, 2, 1, 3)
        k = qkv[:, :, 1].transpose(0, 2, 1, 3)
        v = qkv[:, :, 2].transpose(0, 2, 1, 3)
        scores = jnp.einsum('bhnd,bhmd->bhnm', q, k) * SCALE
        attn = jax.nn.softmax(scores, axis=-1)
        out = jnp.einsum('bhnm,bhmd->bhnd', attn, v)
        out = out.transpose(0, 2, 1, 3).reshape(B, N, C)
        return out @ w_out.T + b_out

    def _L0_ffn_ref(x, gate_w, w1, w2):
        import jax, jax.numpy as jnp
        import numpy as np
        D_MODEL = 256
        D_FF = 512
        NUM_EXPERTS = 16
        TOP_K = 2
        CAPACITY_FACTOR = 1.25
        BATCH, SEQ = (4, 512)
        B, S, d = x.shape
        T = B * S
        E, K = (NUM_EXPERTS, TOP_K)
        capacity = int(CAPACITY_FACTOR * T * K / E)
        xf = x.reshape(T, d)
        logits = xf @ gate_w.T
        probs = jax.nn.sigmoid(logits)
        top_vals, sel = jax.lax.top_k(probs, K)
        weights = top_vals / (top_vals.sum(-1, keepdims=True) + 1e-06)
        flat_sel = sel.reshape(-1)
        onehot = jax.nn.one_hot(flat_sel, E, dtype=jnp.int32)
        ranks = jnp.take_along_axis(jnp.cumsum(onehot, axis=0), flat_sel[:, None], axis=1)[:, 0] - 1
        valid = ranks < capacity
        sentinel = E * capacity
        slot = jnp.where(valid, flat_sel * capacity + ranks, sentinel)
        x_rep = jnp.repeat(xf, K, axis=0)
        padded = jnp.zeros((sentinel + 1, d), xf.dtype).at[slot].set(x_rep)
        padded = padded[:sentinel].reshape(E, capacity, d)
        h = jax.nn.gelu(jnp.einsum('ecd,edf->ecf', padded, w1), approximate=False)
        out_padded = jnp.einsum('ecf,efd->ecd', h, w2).reshape(sentinel, d)
        gathered = out_padded[jnp.minimum(slot, sentinel - 1)]
        gathered = jnp.where(valid[:, None], gathered, jnp.zeros((), xf.dtype))
        out = (gathered * weights.reshape(-1)[:, None]).reshape(T, K, d).sum(axis=1)
        return out.reshape(B, S, d)
    h = _L0_tok_ref(x, L0_tok_weight, L0_tok_bias)
    h = h + _L0_attn_ref(_layernorm(h, axis=-1), L0_attn_w_qkv, L0_attn_b_qkv, L0_attn_w_out, L0_attn_b_out)
    h = h + _L0_ffn_ref(_layernorm(h, axis=-1), L0_ffn_gate_w, L0_ffn_w1, L0_ffn_w2)
    return h

_drawn_inputs = setup_inputs


def setup_inputs(seed=0):
    import zlib

    import numpy as np

    out = dict(_drawn_inputs(seed))
    spreads = {}
    factors = {'L0_attn_b_qkv': 3.524, 'L0_attn_b_out': 4.326}
    for name, (base, spread) in spreads.items():
        noise = np.random.default_rng([zlib.crc32(name.encode()), seed]).standard_normal(out[name].shape)
        drawn = base * np.exp(spread * noise) if base else spread * noise
        out[name] = jnp.asarray(drawn.astype(out[name].dtype))
    for name, factor in factors.items():
        out[name] = (out[name] * factor).astype(out[name].dtype)
    return out
```

```python
from contextlib import ExitStack

import concourse.bass as bass
from concourse import mybir

P = 128
F32 = mybir.dt.float32
BF16 = mybir.dt.bfloat16
I32 = mybir.dt.int32
U32 = mybir.dt.uint32
ALU = mybir.AluOpType
ACT = mybir.ActivationFunctionType
AX = mybir.AxisListType

EPS = 1e-5
HEADS = 16
HD = 16
G = 4
HG = HEADS // G
C = 256
CC = C // P
N = 1024
NT = N // P
E_ = 16
F = 512
FC = F // P
STEPS = 2 * NT * 2
WIN = G * STEPS
LEAD = 40
KQ = 6 * HD
KS = KQ + 3
Q_TERMS = (0, 0, 0, 1, 1, 2)
K_TERMS = (0, 1, 2, 0, 1, 0)
BT_AT = (13, 15, 17, 19)
OP_AT = (22, 27, 29, 33)
XT_AT = (54, 56, 59, 61)
X2T_AT = (77, 79, 81, 83)
GATE_AT, RANK_AT = 86, 109


def small_work(t):
    g, o = t // STEPS, t % STEPS
    if o == 5:
        return "o_turn", g - 1, 1
    if o in (7, 9):
        return "qk", g + 2, (o - 7) // 2
    if o == 11:
        return "v", g + 2, 0
    if o == 20:
        return "o_turn", g, 0
    if o == 25:
        return "max_turn", g + 1, 0
    for name, at, rel in (("on_turn", BT_AT, -1), ("out", OP_AT, -1), ("x_turn", XT_AT, 1), ("x2_turn", X2T_AT, -1)):
        if t in at:
            return name, 4 * rel, at.index(t)
    if t == GATE_AT:
        return "gate", -4, 0
    if t == RANK_AT:
        return "rank", -4, 0
    return None


def is_int(x):
    return isinstance(x, int)


def wait(eng, sem, value, begun=None):
    if not is_int(value) or value > 0:
        if begun is not None and not is_int(value):
            value = eng.to_reg(value)
            eng.wait_ge(begun, 1)
        eng.wait_ge(sem, value)


def attention_and_routing(nc, begun, slot_of, weight_of, dram, NB, CAP):
    SLOTS = E_ * CAP
    ctx = ExitStack()
    with ctx:
        def sb(name, shape, dt=F32):
            return ctx.enter_context(nc.sbuf_tensor(name, shape, dt))

        def sem(name):
            return ctx.enter_context(nc.semaphore(name))

        ident = sb("ident", [P, P])
        ident_bf = sb("ident_bf", [P, P], BF16)
        before_bf = sb("before_bf", [P, P], BF16)
        ones_bf = sb("ones_bf", [P, P], BF16)
        expert_iota = sb("expert_iota", [P, E_])
        minus_half = sb("minus_half", [P, NT])
        zeros = sb("zeros", [P, 1024])
        wqk = sb("wqk", [P, CC, G, P])
        wv = sb("wv", [P, CC, C])
        wo = sb("wo", [P, CC, C])
        gw = sb("gw", [P, CC, E_])
        b_qk = sb("b_qk", [P, G])
        b_v = sb("b_v", [P, C])
        b_o = sb("b_o", [P, C])
        b_tok = sb("b_tok", [P, C])

        tok = sb("tok", [P, NT], I32)
        emb = sb("emb", [P, NT, C])
        stat1 = sb("stat1", [P, NT, 6])
        mv1 = sb("mv1", [P, NT, 2])
        rstd1 = sb("rstd1", [P, NT])
        xn = sb("xn", [P, NT, C])
        xnT = sb("xnT", [P, CC, N])
        qk_full = sb("qk_full", [P, N])
        qk_rest = sb("qk_rest", [P, N])
        qk_part = [sb(f"qk_part{i}", [P, N], BF16) for i in range(3)]
        q_stack = [sb(f"q_stack{g}", [KS, HG * N], BF16) for g in range(G)]
        k_stack = [sb(f"k_stack{g}", [KS, HG * N], BF16) for g in range(G)]
        v_sb = [sb(f"v_sb{g}", [P, NT, HG, 32]) for g in range(G)]
        half_max = sb("half_max", [P, HG * NT, 2])
        neg_max = sb("neg_max", [P, HG * NT])
        neg_rest = sb("neg_rest", [P, HG * NT])
        neg_part = sb("neg_part", [P, 3, HG * NT], BF16)
        max_rows = sb("max_rows", [3 * HG * NT, P], BF16)
        probs = [sb(f"probs{i}", [P, HG, 512]) for i in range(2)]
        oT = sb("oT", [P, 2, 512])
        rsum = sb("rsum", [P, 2, 4 * HG])
        o_n = sb("o_n", [P, NT, C])
        turned = sb("turned", [P, CC, N])
        resid = sb("resid", [P, NT, C])
        h2 = sb("h2", [P, NT, C])
        stat2 = sb("stat2", [P, NT, 6])
        mv2 = sb("mv2", [P, NT, 2])
        rstd2 = sb("rstd2", [P, NT])
        xn2 = sb("xn2", [P, NT, C])
        gate_e = sb("gate_e", [P, NT, E_])
        gate_p = sb("gate_p", [P, NT, E_])
        top8 = sb("top8", [P, NT, 8])
        top8_at = sb("top8_at", [P, NT, 8], U32)
        gsum = sb("gsum", [P, NT])
        weight2 = sb("weight2", [P, NT, 2])
        sel = sb("sel", [P, NT, 2])
        hot = [sb(f"hot{k}", [P, NT, E_]) for k in range(2)]
        hot_bf = sb("hot_bf", [P, NT, E_], BF16)
        carry_bf = sb("carry_bf", [P, E_], BF16)
        hot_sum = sb("hot_sum", [P, E_])
        picked = [sb(f"picked{k}", [P, NT, E_]) for k in range(2)]
        rank = sb("rank", [P, NT, 2])
        valid = sb("valid", [P, NT, 2])
        begun_mark = sb("begun_mark", [P, 1])
        slot = sb("slot", [P, NT, 2])
        slot_at = sb("slot_at", [P, NT, 2], I32)
        var1_sb = sb("var1_sb", [P, NT])
        var2_sb = sb("var2_sb", [P, NT])

        s2_ps = ctx.enter_context(nc.psum_tensor("s2_ps", [P, 2, 2, 512], F32))
        s1_ps = ctx.enter_context(nc.psum_tensor("s1_ps", [P, 2, 512], F32))
        o_ps = ctx.enter_context(nc.psum_tensor("o_ps", [P, 512], F32))
        m_ps = ctx.enter_context(nc.psum_tensor("m_ps", [P, 512], F32))
        m_bf = m_ps[:, :].bitcast(BF16)

        consts = sem("consts")
        loads = sem("loads")
        tok_in = sem("tok_in")
        emb_in = sem("emb_in")
        emb_b = sem("emb_b")
        stats1 = sem("stats1")
        var1 = sem("var1")
        rstd1_s = sem("rstd1_s")
        xn_s = sem("xn_s")
        x_turn = sem("x_turn")
        xT_s = sem("xT_s")
        qk_s = sem("qk_s")
        qk_fulls = sem("qk_fulls")
        qk_out = sem("qk_out")
        split_a = sem("split_a")
        split_b = sem("split_b")
        split_s = sem("split_s")
        stack_in = [sem(f"stack_in{g}") for g in range(G)]
        v_turn = sem("v_turn")
        v_s = sem("v_s")
        s1_s = sem("s1_s")
        s1_max = sem("s1_max")
        neg_s = sem("neg_s")
        max_turn = sem("max_turn")
        max_rows_s = sem("max_rows_s")
        max_in = [sem(f"max_in{g}") for g in range(G)]
        s2_s = sem("s2_s")
        exp_s = sem("exp_s")
        av_s = sem("av_s")
        oT_s = sem("oT_s")
        o_turn = sem("o_turn")
        rsum_s = sem("rsum_s")
        on_s = sem("on_s")
        on_turn = sem("on_turn")
        onT_s = sem("onT_s")
        resid_s = sem("resid_s")
        out_mm = sem("out_mm")
        h2_s = sem("h2_s")
        h2_st = sem("h2_st")
        stats2 = sem("stats2")
        var2 = sem("var2")
        rstd2_s = sem("rstd2_s")
        xn2_s = sem("xn2_s")
        x2_turn = sem("x2_turn")
        x2T_s = sem("x2T_s")
        gate_mm = sem("gate_mm")
        gate_s = sem("gate_s")
        route = sem("route")
        rank_mm = sem("rank_mm")
        picked_s = sem("picked_s")
        route2 = sem("route2")
        slots_s = sem("slots_s")
        sent = sem("sent")
        zeroed = sem("zeroed")
        v_init = sem("v_init")
        ROUTE1, ROUTE2 = 26, 8
        CONSTS = 10 + 2 * G

        def taken(work, w):
            name, lu, part = work
            u, b = w * G + lu, w + lu // G
            return {
                "o_turn": (on_s, u * 2 + part + 1), "qk": (qk_out, u * 2 + part + 1), "v": (v_s, u + 1),
                "max_turn": (max_rows_s, u + 1), "on_turn": (onT_s, b * 4 + part + 1), "out": (h2_s, b * 4 + part + 1),
                "x_turn": (xT_s, b * 4 + part + 1), "x2_turn": (x2T_s, b * 4 + part + 1), "gate": (gate_s, b + 1),
                "rank": (picked_s, b * 2 + 2),
            }[name]

        def windows(eng, window):
            full = (True, True, True)
            flags = lambda w: (w >= 1, 0 <= w < NB, w + 1 < NB)
            window(-1, flags(-1))
            window(0, flags(0))
            if NB > 2:
                with eng.Fori(1, NB - 1) as w:
                    window(w, full)
            window(NB - 1, flags(NB - 1))
            window(NB, flags(NB))

        def here(flags, lu):
            return flags[lu // G + 1]

        with nc.Block() as block:

            @block.sync
            def _(sp):
                for dst, src in ((wqk, dram["wqk"]), (wv, dram["wv"]), (wo, dram["wo"]), (gw, dram["gw"]), (b_qk, dram["b_qk"])):
                    sp.dma_start(dst.ap(), src).then_inc(loads, 16)
                for dst, src in ((b_tok, dram["b_tok"]), (b_v, dram["b_v"]), (b_o, dram["b_o"])):
                    sp.dma_start(dst[:, :], src.rearrange("(a n) -> a n", a=1).broadcast_to((P, C))).then_inc(loads, 16)

                def window(w, flags):
                    prv, cur, nxt = flags
                    for t in range(WIN):
                        g, o = t // STEPS, t % STEPS
                        if t == 0 and nxt:
                            wait(sp, emb_in, (w + 1) * 16 * NT, begun)
                            sp.dma_start(tok[:, :], dram["tok"][w + 1]).then_inc(tok_in, 16)
                        if is_int(w) and w == 0 and o == 1:
                            if g == 0:
                                sp.wait_ge(consts, CONSTS)
                            rows = SLOTS // G
                            sp.dma_start(
                                dram["slots"][g * rows:(g + 1) * rows, :].rearrange("(p r) c -> p r c", p=P),
                                zeros[:, 0:C].unsqueeze(1).broadcast_to((P, rows // P, C)),
                            ).then_inc(zeroed, 16)
                        if o == 14 and here(flags, g + 2):
                            u, gb, b = w * G + g + 2, (g + 2) % G, w + (g + 2) // G
                            wait(sp, split_s, u * 2 + 2, begun)
                            wait(sp, s2_s, (u - G + 1) * STEPS, begun)
                            for n in range(6):
                                sp.dma_start(q_stack[gb][n * HD:(n + 1) * HD, :], qk_part[Q_TERMS[n]][0:64, :]).then_inc(stack_in[gb], 16)
                                sp.dma_start(k_stack[gb][n * HD:(n + 1) * HD, :], qk_part[K_TERMS[n]][64:128, :]).then_inc(stack_in[gb], 16)
                        if o == 26 and here(flags, g + 1):
                            wait(sp, max_rows_s, w * G + g + 2, begun)
                            sp.dma_start(q_stack[(g + 1) % G][KQ:KS, :], max_rows[:, :]).then_inc(max_in[(g + 1) % G], 16)
                        if t == OP_AT[-1] + 2 and prv:
                            wait(sp, h2_s, w * 4, begun)
                            sp.dma_start(dram["h2"][w - 1], h2[:, :, :]).then_inc(h2_st, 16)

                windows(sp, window)
                wait(sp, h2_st, 16 * NB, begun)

            @block.gpsimd
            def _(pool):
                pool.memset(begun_mark[:, :], 0.0).then_inc(begun, 1)
                pool.memset(ident[:, :], 0.0).then_inc(consts, 1)
                pool.memset(ident_bf[:, :], 0.0).then_inc(consts, 1)
                pool.memset(ones_bf[:, :], 1.0).then_inc(consts, 1)
                pool.memset(minus_half[:, :], -0.5).then_inc(consts, 1)
                pool.memset(zeros[:, :], 0.0).then_inc(consts, 1)
                pool.memset(carry_bf[:, :], 0.0).then_inc(consts, 1)
                pool.iota(expert_iota[:, :], pattern=[[1, E_]], base=0, channel_multiplier=0,
                          allow_small_or_imprecise_dtypes=True).then_inc(consts, 1)
                pool.wait_ge(consts, 7)
                for m in (ident, ident_bf):
                    pool.affine_select(out=m[:, :], in_=m[:, :], compare_op=ALU.not_equal, fill=1.0, base=0,
                                       pattern=[[-1, P]], channel_multiplier=1).then_inc(consts, 1)
                pool.affine_select(out=before_bf[:, :], in_=ones_bf[:, :], compare_op=ALU.is_gt, fill=0.0, base=0,
                                   pattern=[[1, P]], channel_multiplier=-1).then_inc(consts, 1)
                for g in range(G):
                    pool.memset(v_sb[g][:, :, :, HD:32], 0.0).then_inc(v_init, 1)
                pool.wait_ge(v_init, G)
                for g in range(G):
                    pool.memset(v_sb[g][:, :, :, HD:HD + 1], 1.0).then_inc(consts, 1)
                pool.wait_ge(consts, 10 + G)
                for g in range(G):
                    pool.memset(k_stack[g][KQ:KS, :], 1.0).then_inc(consts, 1)
                pool.wait_ge(consts, CONSTS)
                pool.wait_ge(loads, 16 * 8)

                def layer_norm(src, mv, var, rstd, dst, stat_done, var_done, rstd_done, out_done, b):
                    wait(pool, stat_done, b * (2 * NT) + 2 * NT, begun)
                    pool.tensor_scalar(var, mv[:, :, 1], EPS, None, ALU.add).then_inc(var_done, 1)
                    wait(pool, var_done, b + 1, begun)
                    pool.tensor_tensor(rstd[:, :], var, minus_half[:, :], ALU.pow).then_inc(rstd_done, 1)
                    wait(pool, rstd_done, b + 1, begun)
                    for n in range(NT):
                        pool.tensor_scalar(dst[:, n, :], src[:, n, :], mv[:, n, 0:1], rstd[:, n:n + 1],
                                           ALU.subtract, ALU.mult).then_inc(out_done, 1)

                def window(w, flags):
                    prv, cur, nxt = flags
                    for t in range(WIN):
                        g, o = t // STEPS, t % STEPS
                        if o in (8, 10) and here(flags, g + 2):
                            half, u = (o - 8) // 2, w * G + g + 2
                            cols = slice(512 * half, 512 * half + 512)
                            wait(pool, qk_fulls, u * 2 + half + 1, begun)
                            wait(pool, qk_out, u * 2 + half + 1, begun)
                            pool.tensor_tensor(qk_rest[:, cols], qk_full[:, cols], qk_part[0][:, cols], ALU.subtract).then_inc(split_a, 1)
                            pool.tensor_tensor(qk_part[1][:, cols], qk_full[:, cols], qk_part[0][:, cols], ALU.subtract).then_inc(split_b, 1)
                            wait(pool, split_a, u * 2 + half + 1, begun)
                            wait(pool, split_b, u * 2 + half + 1, begun)
                            pool.tensor_tensor(qk_part[2][:, cols], qk_rest[:, cols], qk_part[1][:, cols], ALU.subtract).then_inc(split_s, 1)
                        if t == OP_AT[-1] + 3:
                            if prv:
                                wait(pool, x2_turn, (w - 1) * 4, begun)
                                wait(pool, sent, (w - 1) * 16 * 2 * NT, begun)
                                layer_norm(h2, mv2, var2_sb[:, :], rstd2, xn2, stats2, var2, rstd2_s, xn2_s, w - 1)
                            if cur:
                                wait(pool, h2_s, w * 4, begun)
                                pool.tensor_tensor(resid[:, :, :], emb[:, :, :], b_o[:, :].unsqueeze(1).broadcast_to((P, NT, C)),
                                                   ALU.add).then_inc(resid_s, 1)
                            if nxt:
                                wait(pool, tok_in, (w + 1) * 16 + 16, begun)
                                wait(pool, resid_s, w + 1, begun)
                                wait(pool, xn_s, (w + 1) * NT, begun)
                                for n in range(NT):
                                    pool.indirect_dma_start(emb[:, n, :], None, dram["table"],
                                                            bass.IndirectOffsetOnAxis(ap=tok[:, n:n + 1], axis=0)).then_inc(emb_in, 16)
                        if t == 43 and nxt:
                            wait(pool, emb_in, (w + 2) * 16 * NT, begun)
                            pool.tensor_tensor(emb[:, :, :], emb[:, :, :], b_tok[:, :].unsqueeze(1).broadcast_to((P, NT, C)),
                                               ALU.add).then_inc(emb_b, 1)
                        if t == 46 and nxt:
                            wait(pool, x_turn, (w + 1) * 4, begun)
                            layer_norm(emb, mv1, var1_sb[:, :], rstd1, xn, stats1, var1, rstd1_s, xn_s, w + 1)
                        if t == RANK_AT + 5 and prv:
                            wait(pool, slots_s, w, begun)
                            pool.wait_ge(zeroed, 16 * G)
                            for n in range(NT):
                                for k in range(2):
                                    pool.indirect_dma_start(dram["slots"], bass.IndirectOffsetOnAxis(ap=slot_at[:, n, k:k + 1], axis=0),
                                                            xn2[:, n, :], None, bounds_check=SLOTS - 1, oob_is_err=False).then_inc(sent, 16)

                pool.wait_ge(consts, CONSTS)
                windows(pool, window)
                pool.wait_ge(zeroed, 16 * G)
                wait(pool, sent, NB * 16 * 2 * NT, begun)


            @block.scalar
            def _(act):
                def window(w, flags):
                    prv, cur, nxt = flags
                    for t in range(WIN):
                        g, o = t // STEPS, t % STEPS
                        if cur:
                            hp = t % 2
                            act.wait_ge(s2_s, w * WIN + t + 1)
                            if hp == 0:
                                wait(act, av_s, w * (WIN // 2) + t // 2 - 1)
                            act.activation(probs[(t // 2) % 2][:, 2 * hp:2 * hp + 2, :], s2_ps[:, t % 2], ACT.Exp,
                                           scale=HD ** -0.5).then_inc(exp_s, 1)
                        for at, lu, nh in ((18, g, 0), (2, g - 1, 1)):
                            if o == at and here(flags, lu):
                                u = w * G + lu
                                act.wait_ge(av_s, u * NT * 2 + nh * NT + NT)
                                wait(act, o_turn, (u - 1) * 2 + nh + 1)
                                act.activation(oT[:, nh, :], o_ps[:, :], ACT.Copy).then_inc(oT_s, 1)
                        work = small_work(t)
                        if work is None or not here(flags, work[1]):
                            continue
                        name, lu, part = work
                        u, b, gb = w * G + lu, w + lu // G, lu % G
                        b_before, g_before = w + (lu - 1) // G, (lu - 1) % G
                        if name == "qk":
                            cols = slice(512 * part, 512 * part + 512)
                            act.wait_ge(qk_s, u * 2 + part + 1)
                            wait(act, split_s, (u - 1) * 2 + part + 1)
                            act.activation(qk_full[:, cols], m_ps[:, :], ACT.Identity, bias=b_qk[:, gb:gb + 1]).then_inc(qk_fulls, 1)
                            wait(act, stack_in[g_before], (b_before + 1) * 192)
                            act.activation(qk_part[0][:, cols], m_ps[:, :], ACT.Identity, bias=b_qk[:, gb:gb + 1]).then_inc(qk_out, 1)
                        elif name == "max_turn":
                            act.wait_ge(max_turn, u + 1)
                            wait(act, max_in[g_before], (b_before + 1) * 16)
                            act.activation(max_rows[:, :], m_bf[0:3 * HG * NT, 0:P], ACT.Copy).then_inc(max_rows_s, 1)
                        elif name in ("x_turn", "on_turn", "x2_turn"):
                            came, went, dst, free, n = {
                                "x_turn": (x_turn, xT_s, xnT, v_turn, b * G),
                                "on_turn": (on_turn, onT_s, turned, gate_mm, b),
                                "x2_turn": (x2_turn, x2T_s, turned, out_mm, b * 4 + 4),
                            }[name]
                            act.wait_ge(came, b * 4 + part + 1)
                            wait(act, free, n)
                            act.activation(dst[:, :, 2 * P * part:2 * P * part + 2 * P],
                                           m_ps[:, :].rearrange("p (c n) -> p c n", c=CC), ACT.Copy).then_inc(went, 1)
                        elif name == "gate":
                            act.wait_ge(gate_mm, b + 1)
                            wait(act, route, b * ROUTE1)
                            act.activation(gate_e[:, :, :].rearrange("p n e -> p (n e)"), m_ps[:, 0:NT * E_], ACT.Exp,
                                           scale=-1.0).then_inc(gate_s, 1)

                act.wait_ge(loads, 16 * 8)
                windows(act, window)

            @block.vector
            def _(dve):
                def then(ins, s, value):
                    ins.then_inc(s, 1)
                    dve.wait_ge(s, value)

                def statistics(src, stat, mv, stat_done, b):
                    for n in range(NT):
                        dve.bn_stats(stat[:, n, :], src[:, n, :]).then_inc(stat_done, 1)
                    wait(dve, stat_done, b * (2 * NT) + NT, begun)
                    for n in range(NT):
                        dve.bn_aggr(mv[:, n, :], stat[:, n, :]).then_inc(stat_done, 1)

                def choose_experts(b):
                    k = b * ROUTE1
                    dve.wait_ge(gate_s, b + 1)
                    then(dve.tensor_scalar(gate_p[:, :, :], gate_e[:, :, :], 1.0, None, ALU.add), route, k + 1)
                    dve.reciprocal(gate_p[:, :, :], gate_p[:, :, :]).then_inc(route, 1)
                    wait(dve, route, k + 2, begun)
                    for n in range(NT):
                        dve.max(top8[:, n, :], gate_p[:, n, :]).then_inc(route, 1)
                    wait(dve, route, k + 2 + NT, begun)
                    for n in range(NT):
                        dve.max_index(top8_at[:, n, :], top8[:, n, :], gate_p[:, n, :]).then_inc(route, 1)
                    k2 = k + 2 + 2 * NT
                    dve.wait_ge(route, k2)
                    then(dve.tensor_tensor(gsum[:, :], top8[:, :, 0], top8[:, :, 1], ALU.add), route, k2 + 1)
                    then(dve.tensor_scalar(gsum[:, :], gsum[:, :], 1e-6, None, ALU.add), route, k2 + 2)
                    then(dve.reciprocal(gsum[:, :], gsum[:, :]), route, k2 + 3)
                    then(dve.tensor_tensor(weight2[:, :, :], top8[:, :, 0:2], gsum[:, :].unsqueeze(2).broadcast_to((P, NT, 2)),
                                           ALU.mult), route, k2 + 4)
                    then(dve.tensor_copy(sel[:, :, :], top8_at[:, :, 0:2]), route, k2 + 5)
                    for i in range(2):
                        dve.tensor_tensor(hot[i][:, :, :], expert_iota[:, :].unsqueeze(1).broadcast_to((P, NT, E_)),
                                          sel[:, :, i:i + 1].broadcast_to((P, NT, E_)), ALU.is_equal).then_inc(route, 1)
                    dve.wait_ge(route, k2 + 7)
                    wait(dve, rank_mm, b)
                    dve.tensor_tensor(hot_bf[:, :, :], hot[0][:, :, :], hot[1][:, :, :], ALU.add).then_inc(route, 1)

                def give_slots(b):
                    k = b * ROUTE2
                    dve.wait_ge(rank_mm, b + 1)
                    ranks = m_ps[:, 0:NT * E_].rearrange("p (n e) -> p n e", n=NT)
                    for i in range(2):
                        dve.tensor_tensor(picked[i][:, :, :], ranks, hot[i][:, :, :], ALU.mult).then_inc(picked_s, 1)
                    dve.wait_ge(picked_s, b * 2 + 2)
                    for i in range(2):
                        dve.tensor_reduce(rank[:, :, i], picked[i][:, :, :], AX.X, ALU.add).then_inc(route2, 1)
                    dve.tensor_reduce(hot_sum[:, :], hot_bf[:, :, :].rearrange("p n e -> p e n"), AX.X, ALU.add).then_inc(route2, 1)
                    dve.wait_ge(route2, k + 3)
                    then(dve.tensor_tensor(carry_bf[:, :], carry_bf[:, :], hot_sum[:, :], ALU.add), route2, k + 4)
                    then(dve.tensor_scalar(valid[:, :, :], rank[:, :, :], float(CAP), None, ALU.is_lt), route2, k + 5)
                    then(dve.scalar_tensor_tensor(slot[:, :, :], sel[:, :, :], float(CAP), rank[:, :, :], ALU.mult, ALU.add), route2, k + 6)
                    then(dve.scalar_tensor_tensor(slot[:, :, :], slot[:, :, :], float(SLOTS), valid[:, :, :], ALU.subtract, ALU.mult), route2, k + 7)
                    wait(dve, sent, b * 16 * 2 * NT)
                    dve.tensor_scalar(slot_at[:, :, :], slot[:, :, :], float(SLOTS), None, ALU.add).then_inc(slots_s, 1)
                    cols = bass.ds(b * 2 * NT, 2 * NT)
                    dve.tensor_scalar(slot_of[:, cols], slot[:, :, :].rearrange("p n k -> p (n k)"), float(SLOTS), float(SLOTS - 1), ALU.add, ALU.min)
                    dve.tensor_tensor(weight_of[:, cols], weight2[:, :, :].rearrange("p n k -> p (n k)"),
                                      valid[:, :, :].rearrange("p n k -> p (n k)"), ALU.mult).then_inc(route2, 1)
                    dve.wait_ge(route2, k + 8)

                def window(w, flags):
                    prv, cur, nxt = flags
                    for t in range(WIN):
                        g, o = t // STEPS, t % STEPS
                        ahead = t + LEAD
                        lu, step = ahead // STEPS, ahead % STEPS
                        if here(flags, lu):
                            u = w * G + lu
                            if step == 0:
                                wait(dve, neg_s, (u - 1) * 5 + 1)
                            for half in range(2):
                                dve.wait_ge(s1_s, u * 64 + step * 2 + half + 1)
                                dve.tensor_reduce(half_max[:, step, half:half + 1], s1_ps[:, half, :], AX.X, ALU.max).then_inc(s1_max, 1)
                            if step == STEPS - 1:
                                k = u * 5
                                dve.wait_ge(s1_max, u * 64 + 64)
                                then(dve.tensor_reduce(neg_max[:, :], half_max[:, :, :], AX.X, ALU.max, negate=True), neg_s, k + 1)
                                wait(dve, max_turn, u)
                                then(dve.tensor_copy(neg_part[:, 0, :], neg_max[:, :]), neg_s, k + 2)
                                then(dve.tensor_tensor(neg_rest[:, :], neg_max[:, :], neg_part[:, 0, :], ALU.subtract), neg_s, k + 3)
                                then(dve.tensor_copy(neg_part[:, 1, :], neg_rest[:, :]), neg_s, k + 4)
                                dve.tensor_tensor(neg_part[:, 2, :], neg_rest[:, :], neg_part[:, 1, :], ALU.subtract).then_inc(neg_s, 1)
                        if t == OP_AT[-1] + 1 and prv:
                            dve.wait_ge(h2_s, w * 4)
                            wait(dve, xn2_s, (w - 1) * NT)
                            statistics(h2, stat2, mv2, stats2, w - 1)
                        if t == 45 and nxt:
                            dve.wait_ge(emb_b, w + 2)
                            wait(dve, xn_s, (w + 1) * NT)
                            statistics(emb, stat1, mv1, stats1, w + 1)
                        if t == GATE_AT + 1 and prv:
                            choose_experts(w - 1)
                        work = small_work(t)
                        if work is None or not here(flags, work[1]):
                            continue
                        name, lu, part = work
                        u, b, gb = w * G + lu, w + lu // G, lu % G
                        if name == "o_turn":
                            dve.wait_ge(o_turn, u * 2 + part + 1)
                            heads = m_ps[:, :].rearrange("p (n h d) -> p n h d", n=4, h=HG)
                            sums = rsum[:, part, :].rearrange("p (n h) -> p n h", n=4)
                            then(dve.reciprocal(sums, heads[:, :, :, HD]), rsum_s, u * 2 + part + 1)
                            if gb == 0:
                                wait(dve, on_turn, b * 4)
                            dst = o_n[:, 4 * part:4 * part + 4, 64 * gb:64 * gb + 64].rearrange("p n (h d) -> p n h d", h=HG)
                            dve.tensor_tensor(dst, heads[:, :, :, 0:HD], sums.unsqueeze(3).broadcast_to((P, 4, HG, HD)), ALU.mult).then_inc(on_s, 1)
                        elif name == "v":
                            dve.wait_ge(v_turn, u + 1)
                            wait(dve, av_s, (u - G) * 2 * NT + 2 * NT)
                            bias = b_v[:, 64 * gb:64 * gb + 64].rearrange("p (h d) -> p h d", h=HG).unsqueeze(1).broadcast_to((P, NT, HG, HD))
                            dve.tensor_tensor(v_sb[gb][:, :, :, 0:HD], m_ps[:, :].rearrange("p (n h d) -> p n h d", n=NT, h=HG), bias,
                                              ALU.add).then_inc(v_s, 1)
                        elif name == "out":
                            dve.wait_ge(out_mm, b * 4 + part + 1)
                            dve.wait_ge(resid_s, b + 1)
                            if part == 0:
                                wait(dve, h2_st, b * 16)
                                wait(dve, xn2_s, b * NT)
                            dve.tensor_tensor(h2[:, 2 * part:2 * part + 2, :], m_ps[:, :].rearrange("p (n c) -> p n c", n=2),
                                              resid[:, 2 * part:2 * part + 2, :], ALU.add).then_inc(h2_s, 1)
                        elif name == "rank":
                            give_slots(b)

                dve.wait_ge(consts, CONSTS)
                dve.wait_ge(loads, 16 * 8)
                windows(dve, window)

            @block.tensor
            def _(pe):
                def turn4(src, part, done):
                    for c in range(CC):
                        for n in range(2):
                            last = pe.transpose(m_ps[:, (2 * c + n) * P:(2 * c + n + 1) * P],
                                                src[:, 2 * part + n, c * P:(c + 1) * P], ident[:, :])
                    last.then_inc(done, 1)

                def do_small(work, w):
                    name, lu, part = work
                    u, b, gb = w * G + lu, w + lu // G, lu % G
                    if name == "o_turn":
                        pe.wait_ge(oT_s, u * 2 + part + 1)
                        for n in range(4):
                            last = pe.transpose(m_ps[:, n * P:(n + 1) * P], oT[:, part, n * P:(n + 1) * P], ident[:, :])
                        last.then_inc(o_turn, 1)
                    elif name == "qk":
                        if part == 0:
                            pe.wait_ge(xT_s, b * 4 + 4)
                        for c in range(CC):
                            last = pe.matmul(m_ps[:, :], wqk[:, c, gb, :], xnT[:, c, 512 * part:512 * part + 512],
                                             start=(c == 0), stop=(c == CC - 1))
                        last.then_inc(qk_s, 1)
                    elif name == "v":
                        for n in range(NT):
                            for c in range(CC):
                                last = pe.matmul(m_ps[:, 64 * n:64 * n + 64], xnT[:, c, P * n:P * n + P], wv[:, c, 64 * gb:64 * gb + 64],
                                                 start=(c == 0), stop=(c == CC - 1))
                        last.then_inc(v_turn, 1)
                    elif name == "max_turn":
                        pe.wait_ge(neg_s, u * 5 + 5)
                        pe.transpose(m_bf[0:3 * HG * NT, 0:P], neg_part[:, :, :].rearrange("p a n -> p (a n)"), ident_bf[:, :]).then_inc(max_turn, 1)
                    elif name == "on_turn":
                        pe.wait_ge(on_s, b * G * 2 + G * 2)
                        turn4(o_n, part, on_turn)
                    elif name == "x_turn":
                        pe.wait_ge(xn_s, b * NT + 2 * part + 2)
                        turn4(xn, part, x_turn)
                    elif name == "x2_turn":
                        pe.wait_ge(xn2_s, b * NT + 2 * part + 2)
                        turn4(xn2, part, x2_turn)
                    elif name == "out":
                        pe.wait_ge(onT_s, b * 4 + part + 1)
                        for n in range(2):
                            at = (2 * part + n) * P
                            for c in range(CC):
                                last = pe.matmul(m_ps[:, C * n:C * n + C], turned[:, c, at:at + P], wo[:, c, :],
                                                 start=(c == 0), stop=(c == CC - 1))
                        last.then_inc(out_mm, 1)
                    elif name == "gate":
                        pe.wait_ge(x2T_s, b * 4 + 4)
                        for n in range(NT):
                            for c in range(CC):
                                last = pe.matmul(m_ps[:, E_ * n:E_ * n + E_], turned[:, c, P * n:P * n + P], gw[:, c, :],
                                                 start=(c == 0), stop=(c == CC - 1))
                        last.then_inc(gate_mm, 1)
                    elif name == "rank":
                        pe.wait_ge(route, b * ROUTE1 + ROUTE1)
                        wait(pe, route2, b * ROUTE2)
                        flat = hot_bf[:, :, :].rearrange("p n e -> p (n e)")
                        pe.matmul(m_ps[:, 0:NT * E_], before_bf[:, :], flat, start=True, stop=False)
                        for n in range(1, NT):
                            pe.matmul(m_ps[:, n * E_:NT * E_], ones_bf[:, :], flat[:, 0:(NT - n) * E_], start=False, stop=False)
                        pe.matmul(m_ps[:, 0:NT * E_], ones_bf[:, :], carry_bf[:, :].unsqueeze(1).broadcast_to((P, NT, E_)),
                                  start=False, stop=True).then_inc(rank_mm, 1)

                def window(w, flags):
                    prv, cur, nxt = flags
                    before = ("max_turn", 0, 0) if cur else ("o_turn", -1, 0) if prv else None
                    for t in range(WIN):
                        ahead = t + LEAD
                        lu, step = ahead // STEPS, ahead % STEPS
                        if here(flags, lu):
                            u, gb = w * G + lu, lu % G
                            hh, n = step // NT, step % NT
                            if step == 0:
                                pe.wait_ge(stack_in[gb], (w + lu // G + 1) * 192)
                            for half in range(2):
                                wait(pe, s1_max, u * 64 + step * 2 + half - 1)
                                pe.matmul(s1_ps[:, half, :], q_stack[gb][0:KQ, hh * N + n * P:hh * N + n * P + P],
                                          k_stack[gb][0:KQ, hh * N + half * 512:hh * N + half * 512 + 512],
                                          start=True, stop=True).then_inc(s1_s, 1)
                        if cur:
                            g, o = t // STEPS, t % STEPS
                            nh, mt, hp = o // 16, (o % 16) // 2, o % 2
                            if o == 0:
                                pe.wait_ge(max_in[g], (w + 1) * 16)
                            wait(pe, exp_s, w * WIN + t - 1)
                            for i in range(2):
                                hh = 2 * hp + i
                                last = pe.matmul(s2_ps[:, t % 2, i, :], k_stack[g][0:KS, hh * N + mt * P:hh * N + mt * P + P],
                                                 q_stack[g][0:KS, hh * N + nh * 512:hh * N + nh * 512 + 512], start=True, stop=True)
                            last.then_inc(s2_s, 1)
                        lp = (t - 1) // 2 - 1
                        if t % 2 == 1 and (cur if lp >= 0 else prv):
                            q = w * (WIN // 2) + lp
                            g, mt = (lp // 16) % G, lp % NT
                            pe.wait_ge(exp_s, q * 2 + 2)
                            if lp % 16 == 0:
                                pe.wait_ge(v_s, w * G + g + 1)
                            if mt == 0:
                                wait(pe, oT_s, w * (2 * G) + lp // NT)
                            for hh in range(HG):
                                last = pe.matmul(o_ps[32 * hh:32 * hh + 32, :], v_sb[g][:, mt, hh, :], probs[lp % 2][:, hh, :],
                                                 start=(mt == 0), stop=(mt == NT - 1))
                            last.then_inc(av_s, 1)
                        work = small_work(t)
                        if work is not None and here(flags, work[1]):
                            if before is not None:
                                wait(pe, *taken(before, w))
                            do_small(work, w)
                            before = work

                pe.wait_ge(consts, CONSTS)
                pe.wait_ge(loads, 16 * 8)
                windows(pe, window)


def experts(nc, begun, dram, CAP):
    TE = 5
    ST = CAP // TE
    SB = ST // P
    YB = (SB + 1) // 2
    PAIRS = E_ // 2
    NI = E_ * TE
    assert ST * TE == CAP and SB * P == ST and ST <= 512
    ctx = ExitStack()
    with ctx:
        def sb(name, shape, dt=F32):
            return ctx.enter_context(nc.sbuf_tensor(name, shape, dt))

        def sem(name):
            return ctx.enter_context(nc.semaphore(name))

        ident = sb("x_ident", [P, P])
        w1 = [sb(f"w1_{i}", [P, CC, F]) for i in range(2)]
        w2 = [sb(f"w2_{i}", [P, FC, C]) for i in range(2)]
        rows = [sb(f"rows{i}", [P, SB, C]) for i in range(2)]
        rowsT = [sb(f"rowsT{i}", [P, CC, ST]) for i in range(2)]
        hid = [sb(f"hid{i}", [P, FC, ST]) for i in range(2)]
        y = [sb(f"y{i}", [P, SB, C]) for i in range(2)]
        turn_ps = ctx.enter_context(nc.psum_tensor("turn_ps", [P, CC, 512], F32))
        hid_ps = ctx.enter_context(nc.psum_tensor("hid_ps", [P, FC, 512], F32))
        y_ps = ctx.enter_context(nc.psum_tensor("y_ps", [P, 2, 512], F32))

        mask = sem("x_mask")
        w_in = [sem(f"w_in{i}") for i in range(2)]
        rows_in = [sem(f"rows_in{i}") for i in range(2)]
        turn_mm = sem("turn_mm")
        rowsT_s = sem("rowsT_s")
        hid_mm = sem("hid_mm")
        hid_s = sem("hid_s")
        y_mm = sem("y_mm")
        y_s = sem("y_s")
        y_st = [sem(f"y_st{i}") for i in range(2)]

        def pairs(eng, body):
            body(0, True, False)
            with eng.Fori(1, PAIRS - 1) as j:
                body(j, False, False)
            body(PAIRS - 1, False, True)

        with nc.Block() as block:

            @block.gpsimd
            def _(pool):
                pool.memset(ident[:, :], 0.0).then_inc(mask, 1)
                pool.wait_ge(mask, 1)
                pool.affine_select(out=ident[:, :], in_=ident[:, :], compare_op=ALU.not_equal, fill=1.0, base=0,
                                   pattern=[[-1, P]], channel_multiplier=1).then_inc(mask, 1)

            @block.sync
            def _(sp):
                def load_rows(i, par):
                    sp.dma_start(rows[par][:, :, :], dram["slots_t"][i]).then_inc(rows_in[par], 16)

                def load_w(e, par):
                    sp.dma_start(w1[par][:, :, :], dram["w1"][e]).then_inc(w_in[par], 16)
                    sp.dma_start(w2[par][:, :, :], dram["w2"][e]).then_inc(w_in[par], 16)

                load_rows(0, 0)
                load_w(0, 0)
                load_rows(1, 1)

                def body(j, first, last):
                    for k in range(2 * TE):
                        i = j * (2 * TE) + k
                        if not (last and k >= 2 * TE - 2):
                            wait(sp, turn_mm, i + 1, begun)
                            load_rows(i + 2, k % 2)
                        if k % TE == 1 and not (last and k > TE):
                            wait(sp, y_mm, (i - 1) * YB, begun)
                            load_w(j * 2 + k // TE + 1, (k // TE + 1) % 2)
                        wait(sp, y_s, i * YB + YB, begun)
                        sp.dma_start(dram["outs_t"][i], y[k % 2][:, :, :]).then_inc(y_st[k % 2], 16)

                pairs(sp, body)
                for par in range(2):
                    wait(sp, y_st[par], 16 * NI // 2, begun)

            @block.scalar
            def _(act):
                def body(j, first, last):
                    for k in range(2 * TE):
                        i = j * (2 * TE) + k
                        wait(act, y_mm, (i - 1) * YB)
                        for f in range(FC):
                            act.wait_ge(hid_mm, i * FC + f + 1)
                            act.activation(hid[k % 2][:, f, :], hid_ps[:, f, 0:ST], ACT.Gelu).then_inc(hid_s, 1)

                pairs(act, body)

            @block.vector
            def _(dve):
                def copy_turned(i, par):
                    dve.wait_ge(turn_mm, i + 1)
                    wait(dve, hid_mm, (i - 1) * FC)
                    dve.tensor_copy(rowsT[par][:, :, :], turn_ps[:, :, 0:ST]).then_inc(rowsT_s, 1)

                def body(j, first, last):
                    for k in range(2 * TE):
                        i = j * (2 * TE) + k
                        if not (last and k == 2 * TE - 1):
                            copy_turned(i + 1, (k + 1) % 2)
                        if not (first and k == 0):
                            wait(dve, y_st[(k - 1) % 2], stored_before(j, k - 1) * 16)
                            for q in range(YB):
                                n = min(2, SB - 2 * q)
                                dve.wait_ge(y_mm, (i - 1) * YB + q + 1)
                                dve.tensor_copy(y[(k - 1) % 2][:, 2 * q:2 * q + n, :],
                                                y_ps[:, q, 0:n * C].rearrange("p (n c) -> p n c", n=n)).then_inc(y_s, 1)

                def stored_before(j, k):
                    return j * TE + (k // 2)

                copy_turned(0, 0)
                pairs(dve, body)
                k = 2 * TE - 1
                dve.wait_ge(y_st[k % 2], stored_before(PAIRS - 1, k) * 16)
                for q in range(YB):
                    n = min(2, SB - 2 * q)
                    dve.wait_ge(y_mm, (NI - 1) * YB + q + 1)
                    dve.tensor_copy(y[k % 2][:, 2 * q:2 * q + n, :], y_ps[:, q, 0:n * C].rearrange("p (n c) -> p n c", n=n)).then_inc(y_s, 1)

            @block.tensor
            def _(pe):
                def turn(i, par, nth):
                    pe.wait_ge(rows_in[par], nth * 16)
                    wait(pe, rowsT_s, i)
                    for c in range(CC):
                        for n in range(SB):
                            last = pe.transpose(turn_ps[:, c, n * P:(n + 1) * P], rows[par][:, n, c * P:(c + 1) * P], ident[:, :])
                    last.then_inc(turn_mm, 1)

                def first_product(i, par, e_par):
                    pe.wait_ge(rowsT_s, i + 1)
                    for f in range(FC):
                        wait(pe, hid_s, (i - 1) * FC + f + 1)
                        for c in range(CC):
                            last = pe.matmul(hid_ps[:, f, 0:ST], w1[e_par][:, c, f * P:(f + 1) * P], rowsT[par][:, c, :],
                                             start=(c == 0), stop=(c == CC - 1))
                        last.then_inc(hid_mm, 1)

                def second_product(i, par, e_par):
                    pe.wait_ge(hid_s, i * FC + FC)
                    for q in range(YB):
                        wait(pe, y_s, (i - 1) * YB + q + 1)
                        for n in range(2 * q, min(2 * q + 2, SB)):
                            for f in range(FC):
                                last = pe.matmul(y_ps[:, q, (n % 2) * C:(n % 2) * C + C], hid[par][:, f, n * P:(n + 1) * P], w2[e_par][:, f, :],
                                                 start=(f == 0), stop=(f == FC - 1))
                        last.then_inc(y_mm, 1)

                def body(j, first, last):
                    for k in range(2 * TE):
                        i = j * (2 * TE) + k
                        if k % TE == 0:
                            pe.wait_ge(w_in[k // TE], (j + 1) * 32)
                        first_product(i, k % 2, k // TE)
                        if not (last and k == 2 * TE - 1):
                            nth = j * TE + (k + 1) // 2 + 1
                            turn(i + 1, (k + 1) % 2, nth)
                        if not (first and k == 0):
                            second_product(i - 1, (k - 1) % 2, ((k - 1) // TE) % 2)

                pe.wait_ge(mask, 2)
                turn(0, 0, 1)
                pairs(pe, body)
                second_product(NI - 1, 1, 1)


def combine(nc, begun, slot_of, weight_of, dram, NB):
    H = 2
    T = NT // H
    ctx = ExitStack()
    with ctx:
        def sb(name, shape, dt=F32):
            return ctx.enter_context(nc.sbuf_tensor(name, shape, dt))

        def sem(name):
            return ctx.enter_context(nc.semaphore(name))

        at = [sb(f"at{h}", [P, T * 2], I32) for h in range(H)]
        got = [sb(f"got{h}", [P, T, 2, C]) for h in range(H)]
        acc = [sb(f"acc{h}", [P, T, C]) for h in range(H)]
        at_s = sem("at_s")
        got_in = [sem(f"got_in{h}") for h in range(H)]
        acc_in = [sem(f"acc_in{h}") for h in range(H)]
        one_s = sem("one_s")
        acc_s = sem("acc_s")
        out_st = [sem(f"out_st{h}") for h in range(H)]

        def rows(eng, body):
            body(0)
            with eng.Fori(1, NB) as b:
                body(b)

        with nc.Block() as block:

            @block.sync
            def _(sp):
                def load(b):
                    for h in range(H):
                        wait(sp, out_st[h], b * 16, begun)
                        sp.dma_start(acc[h][:, :, :], dram["h2"][b][:, h * T:(h + 1) * T, :]).then_inc(acc_in[h], 16)

                rows(sp, load)

            @block.gpsimd
            def _(pool):
                def fetch(b):
                    for h in range(H):
                        wait(pool, got_in[h], b * 16 * 2 * T, begun)
                        cols = bass.ds(b * (2 * NT) + h * 2 * T, 2 * T)
                        pool.tensor_copy(at[h][:, :], slot_of[:, cols]).then_inc(at_s, 1)
                        wait(pool, at_s, b * H + h + 1, begun)
                        wait(pool, acc_s, (b * H + h - H + 1) * T, begun)
                        for n in range(T):
                            for k in range(2):
                                i = 2 * n + k
                                pool.indirect_dma_start(got[h][:, n, k, :], None, dram["outs"],
                                                        bass.IndirectOffsetOnAxis(ap=at[h][:, i:i + 1], axis=0)).then_inc(got_in[h], 16)

                rows(pool, fetch)

            @block.vector
            def _(dve):
                def add(b):
                    for h in range(H):
                        dve.wait_ge(got_in[h], (b + 1) * 16 * 2 * T)
                        dve.wait_ge(acc_in[h], (b + 1) * 16)
                        for k, done in ((0, one_s), (1, acc_s)):
                            for n in range(T):
                                col = b * (2 * NT) + (h * T + n) * 2 + k
                                dve.scalar_tensor_tensor(acc[h][:, n, :], got[h][:, n, k, :], weight_of[:, bass.ds(col, 1)], acc[h][:, n, :],
                                                         ALU.mult, ALU.add).then_inc(done, 1)
                            if k == 0:
                                dve.wait_ge(one_s, (b * H + h + 1) * T)

                rows(dve, add)

            @block.scalar
            def _(act):
                def store(b):
                    for h in range(H):
                        act.wait_ge(acc_s, (b * H + h + 1) * T)
                        act.dma_start(dram["out"][b][:, h * T:(h + 1) * T, :], acc[h][:, :, :]).then_inc(out_st[h], 16)

                rows(act, store)
                for h in range(H):
                    act.wait_ge(out_st[h], NB * 16)


def lm_tower(nc, a, NB):
    CAP = int(1.25 * NB * N * 2 / E_)
    SLOTS = E_ * CAP
    ST = CAP // 5
    h2 = nc.dram_tensor("h2_rows", (NB * N, C), F32).ap()
    slots = nc.dram_tensor("slot_rows", (SLOTS, C), F32).ap()
    outs = nc.dram_tensor("expert_rows", (SLOTS, C), F32).ap()
    by_row = lambda x: x.rearrange("(b n p) c -> b p n c", p=P, n=NT)
    dram = {
        "table": a["table"], "tok": a["tok"],
        "wqk": a["wqk"], "wv": a["wv"], "wo": a["wo"], "gw": a["gate"],
        "b_qk": a["b_qk"], "b_v": a["b_v"], "b_o": a["b_o"], "b_tok": a["b_tok"],
        "w1": a["w1"].rearrange("e (c p) f -> e p c f", p=P), "w2": a["w2"].rearrange("e (c p) d -> e p c d", p=P),
        "h2": by_row(h2), "out": by_row(a["out"]), "slots": slots, "outs": outs,
        "slots_t": slots.rearrange("(i n p) c -> i p n c", p=P, n=ST // P),
        "outs_t": outs.rearrange("(i n p) c -> i p n c", p=P, n=ST // P),
    }
    with ExitStack() as ctx:
        begun = ctx.enter_context(nc.semaphore("begun"))
        slot_of = ctx.enter_context(nc.sbuf_tensor("slot_of", [P, NB * 2 * NT], I32))
        weight_of = ctx.enter_context(nc.sbuf_tensor("weight_of", [P, NB * 2 * NT], F32))
        attention_and_routing(nc, begun, slot_of, weight_of, dram, NB, CAP)
        experts(nc, begun, dram, CAP)
        combine(nc, begun, slot_of, weight_of, dram, NB)


def lay_out(x, L0_tok_weight, L0_tok_bias, L0_attn_w_qkv, L0_attn_b_qkv, L0_attn_w_out, L0_attn_b_out,
            L0_ffn_gate_w, L0_ffn_w1, L0_ffn_w2):
    import numpy as np

    arr = lambda v: np.ascontiguousarray(np.asarray(v))
    by_chunk = lambda w: arr(np.asarray(w).T.reshape(CC, P, -1).transpose(1, 0, 2))
    nb = x.shape[0]
    w, b = np.asarray(L0_attn_w_qkv), np.asarray(L0_attn_b_qkv)
    qk_rows = np.array([[s * C + (g * HG + h) * HD + d for s in range(2) for d in range(HD) for h in range(HG)] for g in range(G)])
    return {
        "tok": arr(np.asarray(x).reshape(nb, NT, P).transpose(0, 2, 1)),
        "table": arr(np.asarray(L0_tok_weight).T),
        "wqk": arr(w[qk_rows.reshape(-1)].T.reshape(CC, P, G, P).transpose(1, 0, 2, 3)),
        "wv": by_chunk(w[2 * C:3 * C]), "wo": by_chunk(L0_attn_w_out), "gate": by_chunk(L0_ffn_gate_w),
        "b_qk": arr(b[qk_rows].T), "b_v": arr(b[2 * C:3 * C]), "b_o": arr(L0_attn_b_out), "b_tok": arr(L0_tok_bias),
        "w1": arr(L0_ffn_w1), "w2": arr(L0_ffn_w2),
    }


def kernel(**inputs):
    import numpy as np
    import concourse.bacc as bacc
    from concourse.bass_utils import run_bass_kernel_spmd

    nb = inputs["x"].shape[0]
    arrays = lay_out(**inputs)
    nc = bacc.Bacc("TRN2", target_bir_lowering=False, num_devices=1)
    a = {name: nc.dram_tensor("in_" + name, v.shape, mybir.dt.from_np(v.dtype), kind="ExternalInput").ap() for name, v in arrays.items()}
    a["out"] = nc.dram_tensor("out_rows", (nb * N, C), F32, kind="ExternalOutput").ap()
    lm_tower(nc, a, nb)
    r = run_bass_kernel_spmd(nc, [{"in_" + name: v for name, v in arrays.items()}], core_ids=[0])
    return np.asarray(r.results[0]["out_rows"]).reshape(nb, N, C)
```

```python
from contextlib import ExitStack

import concourse.bass as bass
from concourse import mybir

P = 128
F32 = mybir.dt.float32
F32R = mybir.dt.float32r
BF16 = mybir.dt.bfloat16
I32 = mybir.dt.int32
U32 = mybir.dt.uint32
ALU = mybir.AluOpType
ACT = mybir.ActivationFunctionType
AX = mybir.AxisListType

EPS = 1e-5
HEADS = 16
HD = 16
G = 4
HG = HEADS // G
C = 256
CC = C // P
N = 1024
NT = N // P
E_ = 16
F = 512
FC = F // P
STEPS = 2 * NT * 2
WIN = G * STEPS
LEAD = 40
KQ = 6 * HD
KS = KQ + 3
Q_TERMS = (0, 0, 0, 1, 1, 2)
K_TERMS = (0, 1, 2, 0, 1, 0)
SC = 2 * STEPS
RING = tuple(i % 3 for i in range(SC - 1)) + (1,)
BT_AT = (14, 16, 18, 20)
OP_AT = (24, 28, 30, 32)
XT_AT = (56, 60, 62, 64)
X2T_AT = (78, 80, 82, 84)
GATE_AT, RANK_AT = 88, 110


def small_work(t):
    if t < 0:
        return None
    g, o = t // STEPS, t % STEPS
    if o == 6:
        return "o_turn", g - 1, 1
    if o in (8, 10):
        return "qk", g + 2, (o - 8) // 2
    if o == 12:
        return "v", g + 2, 0
    if o == 22:
        return "o_turn", g, 0
    if o == 26:
        return "max_turn", g + 1, 0
    for name, at, rel in (("on_turn", BT_AT, -1), ("out", OP_AT, -1), ("x_turn", XT_AT, 1), ("x2_turn", X2T_AT, -1)):
        if t in at:
            return name, 4 * rel, at.index(t)
    if t == GATE_AT:
        return "gate", -4, 0
    if t == RANK_AT:
        return "rank", -4, 0
    return None


def bank_user_before(i):
    return max(k for k in range(i - SC, i) if RING[k % SC] == RING[i])


def is_int(x):
    return isinstance(x, int)


def wait(eng, sem, value, begun=None):
    if not is_int(value) or value > 0:
        if begun is not None and not is_int(value):
            value = eng.to_reg(value)
            eng.wait_ge(begun, 1)
        eng.wait_ge(sem, value)


def attention_and_routing(nc, begun, slot_of, weight_of, dram, NB, CAP):
    SLOTS = E_ * CAP
    ctx = ExitStack()
    with ctx:
        def sb(name, shape, dt=F32):
            return ctx.enter_context(nc.sbuf_tensor(name, shape, dt))

        def sem(name):
            return ctx.enter_context(nc.semaphore(name))

        ident = sb("ident", [P, P])
        ident_bf = sb("ident_bf", [P, P], BF16)
        before_bf = sb("before_bf", [P, P], BF16)
        ones_bf = sb("ones_bf", [P, P], BF16)
        expert_iota = sb("expert_iota", [P, E_])
        minus_half = sb("minus_half", [P, NT])
        zeros = sb("zeros", [P, 1024])
        wqk = sb("wqk", [P, CC, G, P])
        wv = sb("wv", [P, CC, C])
        wo = sb("wo", [P, CC, C])
        gw = sb("gw", [P, CC, E_])
        b_qk = sb("b_qk", [P, G])
        b_v = sb("b_v", [P, C])
        b_o = sb("b_o", [P, C])
        b_tok = sb("b_tok", [P, C])

        tok = sb("tok", [P, NT], I32)
        emb = sb("emb", [P, NT, C])
        stat1 = sb("stat1", [P, NT, 6])
        mv1 = sb("mv1", [P, NT, 2])
        rstd1 = sb("rstd1", [P, NT])
        xn = sb("xn", [P, NT, C])
        xnT = sb("xnT", [P, CC, N])
        qk_full = sb("qk_full", [P, N])
        qk_rest = sb("qk_rest", [P, N])
        qk_part = [sb(f"qk_part{i}", [P, N], BF16) for i in range(3)]
        q_stack = [sb(f"q_stack{g}", [KS, HG * N], BF16) for g in range(G)]
        k_stack = [sb(f"k_stack{g}", [KS, HG * N], BF16) for g in range(G)]
        v_sb = [sb(f"v_sb{g}", [P, NT, HG, 32]) for g in range(G)]
        half_max = sb("half_max", [P, HG * NT, 2])
        neg_max = sb("neg_max", [P, HG * NT])
        neg_rest = sb("neg_rest", [P, HG * NT])
        neg_part = sb("neg_part", [P, 3, HG * NT], BF16)
        max_rows = sb("max_rows", [3 * HG * NT, P], BF16)
        probs = [sb(f"probs{i}", [P, HG, 512]) for i in range(2)]
        oT = sb("oT", [P, 2, 512])
        rsum = sb("rsum", [P, 2, 4 * HG])
        o_n = sb("o_n", [P, NT, C])
        turned = sb("turned", [P, CC, N])
        resid = sb("resid", [P, NT, C])
        h2 = sb("h2", [P, NT, C])
        stat2 = sb("stat2", [P, NT, 6])
        mv2 = sb("mv2", [P, NT, 2])
        rstd2 = sb("rstd2", [P, NT])
        xn2 = sb("xn2", [P, NT, C])
        gate_e = sb("gate_e", [P, NT, E_])
        gate_p = sb("gate_p", [P, NT, E_])
        top8 = sb("top8", [P, NT, 8])
        top8_at = sb("top8_at", [P, NT, 8], U32)
        gsum = sb("gsum", [P, NT])
        weight2 = sb("weight2", [P, NT, 2])
        sel = sb("sel", [P, NT, 2])
        hot = [sb(f"hot{k}", [P, NT, E_]) for k in range(2)]
        hot_bf = sb("hot_bf", [P, NT, E_], BF16)
        carry_bf = sb("carry_bf", [P, E_], BF16)
        hot_sum = sb("hot_sum", [P, E_])
        picked = [sb(f"picked{k}", [P, NT, E_]) for k in range(2)]
        rank = sb("rank", [P, NT, 2])
        valid = sb("valid", [P, NT, 2])
        begun_mark = sb("begun_mark", [P, 1])
        slot = sb("slot", [P, NT, 2])
        slot_at = sb("slot_at", [P, NT, 2], I32)
        var1_sb = sb("var1_sb", [P, NT])
        var2_sb = sb("var2_sb", [P, NT])

        s2_ps = ctx.enter_context(nc.psum_tensor("s2_ps", [P, 3, 512], F32))
        s1_ps = ctx.enter_context(nc.psum_tensor("s1_ps", [P, 3, 512], F32))
        o_ps = ctx.enter_context(nc.psum_tensor("o_ps", [P, 512], F32))
        m_ps = ctx.enter_context(nc.psum_tensor("m_ps", [P, 512], F32))
        m_bf = m_ps[:, :].bitcast(BF16)

        consts = sem("consts")
        loads = sem("loads")
        tok_in = sem("tok_in")
        emb_in = sem("emb_in")
        emb_b = sem("emb_b")
        stats1 = sem("stats1")
        var1 = sem("var1")
        rstd1_s = sem("rstd1_s")
        xn_s = sem("xn_s")
        x_turn = sem("x_turn")
        xT_s = sem("xT_s")
        qk_s = sem("qk_s")
        qk_fulls = sem("qk_fulls")
        qk_out = sem("qk_out")
        split_a = sem("split_a")
        split_b = sem("split_b")
        split_s = sem("split_s")
        stack_in = [sem(f"stack_in{g}") for g in range(G)]
        v_turn = sem("v_turn")
        v_s = sem("v_s")
        s1_s = sem("s1_s")
        s1_max = sem("s1_max")
        neg_s = sem("neg_s")
        max_turn = sem("max_turn")
        max_rows_s = sem("max_rows_s")
        max_in = [sem(f"max_in{g}") for g in range(G)]
        s2_s = sem("s2_s")
        exp_s = sem("exp_s")
        av_s = sem("av_s")
        oT_s = sem("oT_s")
        o_turn = sem("o_turn")
        rsum_s = sem("rsum_s")
        on_s = sem("on_s")
        on_turn = sem("on_turn")
        onT_s = sem("onT_s")
        resid_s = sem("resid_s")
        out_mm = sem("out_mm")
        h2_s = sem("h2_s")
        h2_st = sem("h2_st")
        stats2 = sem("stats2")
        var2 = sem("var2")
        rstd2_s = sem("rstd2_s")
        xn2_s = sem("xn2_s")
        x2_turn = sem("x2_turn")
        x2T_s = sem("x2T_s")
        gate_mm = sem("gate_mm")
        gate_s = sem("gate_s")
        route = sem("route")
        rank_mm = sem("rank_mm")
        picked_s = sem("picked_s")
        route2 = sem("route2")
        slots_s = sem("slots_s")
        sent = sem("sent")
        zeroed = sem("zeroed")
        v_init = sem("v_init")
        ROUTE1, ROUTE2 = 26, 8
        CONSTS = 10 + 2 * G

        def taken(work, w):
            name, lu, part = work
            u, b = w * G + lu, w + lu // G
            return {
                "o_turn": (on_s, u * 2 + part + 1), "qk": (qk_out, u * 2 + part + 1), "v": (v_s, u + 1),
                "max_turn": (max_rows_s, u + 1), "on_turn": (onT_s, b * 4 + part + 1), "out": (h2_s, b * 4 + part + 1),
                "x_turn": (xT_s, b * 4 + part + 1), "x2_turn": (x2T_s, b * 4 + part + 1), "gate": (gate_s, b + 1),
                "rank": (picked_s, b * 2 + 2),
            }[name]

        def windows(eng, window):
            full = (True, True, True)
            flags = lambda w: (w >= 1, 0 <= w < NB, w + 1 < NB)
            window(-1, flags(-1))
            window(0, flags(0))
            if NB > 2:
                with eng.Fori(1, NB - 1) as w:
                    window(w, full)
            window(NB - 1, flags(NB - 1))
            window(NB, flags(NB))

        def here(flags, lu):
            return flags[lu // G + 1]

        with nc.Block() as block:

            @block.sync
            def _(sp):
                for dst, src in ((wqk, dram["wqk"]), (wv, dram["wv"]), (wo, dram["wo"]), (gw, dram["gw"]), (b_qk, dram["b_qk"])):
                    sp.dma_start(dst.ap(), src).then_inc(loads, 16)
                for dst, src in ((b_tok, dram["b_tok"]), (b_v, dram["b_v"]), (b_o, dram["b_o"])):
                    sp.dma_start(dst[:, :], src.rearrange("(a n) -> a n", a=1).broadcast_to((P, C))).then_inc(loads, 16)

                def window(w, flags):
                    prv, cur, nxt = flags
                    for t in range(WIN):
                        g, o = t // STEPS, t % STEPS
                        if t == 0 and nxt:
                            wait(sp, emb_in, (w + 1) * 16 * NT, begun)
                            sp.dma_start(tok[:, :], dram["tok"][w + 1]).then_inc(tok_in, 16)
                        if is_int(w) and w == 0 and o == 1:
                            if g == 0:
                                sp.wait_ge(consts, CONSTS)
                            rows = SLOTS // G
                            sp.dma_start(
                                dram["slots"][g * rows:(g + 1) * rows, :].rearrange("(p r) c -> p r c", p=P),
                                zeros[:, 0:C].unsqueeze(1).broadcast_to((P, rows // P, C)),
                            ).then_inc(zeroed, 16)
                        if o == 14 and here(flags, g + 2):
                            u, gb, b = w * G + g + 2, (g + 2) % G, w + (g + 2) // G
                            wait(sp, split_s, u * 2 + 2, begun)
                            wait(sp, s2_s, (u - G + 1) * SC, begun)
                            for n in range(6):
                                sp.dma_start(q_stack[gb][n * HD:(n + 1) * HD, :], qk_part[Q_TERMS[n]][0:64, :]).then_inc(stack_in[gb], 16)
                                sp.dma_start(k_stack[gb][n * HD:(n + 1) * HD, :], qk_part[K_TERMS[n]][64:128, :]).then_inc(stack_in[gb], 16)
                        if o == 27 and here(flags, g + 1):
                            wait(sp, max_rows_s, w * G + g + 2, begun)
                            sp.dma_start(q_stack[(g + 1) % G][KQ:KS, :], max_rows[:, :]).then_inc(max_in[(g + 1) % G], 16)
                        if t == OP_AT[-1] + 2 and prv:
                            wait(sp, h2_s, w * 4, begun)
                            sp.dma_start(dram["h2"][w - 1], h2[:, :, :]).then_inc(h2_st, 16)

                windows(sp, window)
                wait(sp, h2_st, 16 * NB, begun)

            @block.gpsimd
            def _(pool):
                pool.memset(begun_mark[:, :], 0.0).then_inc(begun, 1)
                pool.memset(ident[:, :], 0.0).then_inc(consts, 1)
                pool.memset(ident_bf[:, :], 0.0).then_inc(consts, 1)
                pool.memset(ones_bf[:, :], 1.0).then_inc(consts, 1)
                pool.memset(minus_half[:, :], -0.5).then_inc(consts, 1)
                pool.memset(zeros[:, :], 0.0).then_inc(consts, 1)
                pool.memset(carry_bf[:, :], 0.0).then_inc(consts, 1)
                pool.iota(expert_iota[:, :], pattern=[[1, E_]], base=0, channel_multiplier=0,
                          allow_small_or_imprecise_dtypes=True).then_inc(consts, 1)
                pool.wait_ge(consts, 7)
                for m in (ident, ident_bf):
                    pool.affine_select(out=m[:, :], in_=m[:, :], compare_op=ALU.not_equal, fill=1.0, base=0,
                                       pattern=[[-1, P]], channel_multiplier=1).then_inc(consts, 1)
                pool.affine_select(out=before_bf[:, :], in_=ones_bf[:, :], compare_op=ALU.is_gt, fill=0.0, base=0,
                                   pattern=[[1, P]], channel_multiplier=-1).then_inc(consts, 1)
                for g in range(G):
                    pool.memset(v_sb[g][:, :, :, HD:32], 0.0).then_inc(v_init, 1)
                pool.wait_ge(v_init, G)
                for g in range(G):
                    pool.memset(v_sb[g][:, :, :, HD:HD + 1], 1.0).then_inc(consts, 1)
                pool.wait_ge(consts, 10 + G)
                for g in range(G):
                    pool.memset(k_stack[g][KQ:KS, :], 1.0).then_inc(consts, 1)
                pool.wait_ge(consts, CONSTS)
                pool.wait_ge(loads, 16 * 8)

                def layer_norm(src, mv, var, rstd, dst, stat_done, var_done, rstd_done, out_done, b):
                    wait(pool, stat_done, b * (2 * NT) + 2 * NT, begun)
                    pool.tensor_scalar(var, mv[:, :, 1], EPS, None, ALU.add).then_inc(var_done, 1)
                    wait(pool, var_done, b + 1, begun)
                    pool.tensor_tensor(rstd[:, :], var, minus_half[:, :], ALU.pow).then_inc(rstd_done, 1)
                    wait(pool, rstd_done, b + 1, begun)
                    for n in range(NT):
                        pool.tensor_scalar(dst[:, n, :], src[:, n, :], mv[:, n, 0:1], rstd[:, n:n + 1],
                                           ALU.subtract, ALU.mult).then_inc(out_done, 1)

                def window(w, flags):
                    prv, cur, nxt = flags
                    for t in range(WIN):
                        g, o = t // STEPS, t % STEPS
                        if o in (9, 11) and here(flags, g + 2):
                            half, u = (o - 9) // 2, w * G + g + 2
                            cols = slice(512 * half, 512 * half + 512)
                            wait(pool, qk_fulls, u * 2 + half + 1, begun)
                            wait(pool, qk_out, u * 2 + half + 1, begun)
                            pool.tensor_tensor(qk_rest[:, cols], qk_full[:, cols], qk_part[0][:, cols], ALU.subtract).then_inc(split_a, 1)
                            pool.tensor_tensor(qk_part[1][:, cols], qk_full[:, cols], qk_part[0][:, cols], ALU.subtract).then_inc(split_b, 1)
                            wait(pool, split_a, u * 2 + half + 1, begun)
                            wait(pool, split_b, u * 2 + half + 1, begun)
                            pool.tensor_tensor(qk_part[2][:, cols], qk_rest[:, cols], qk_part[1][:, cols], ALU.subtract).then_inc(split_s, 1)
                        if t == OP_AT[-1] + 3:
                            if cur:
                                wait(pool, h2_s, w * 4, begun)
                                pool.tensor_tensor(resid[:, :, :], emb[:, :, :], b_o[:, :].unsqueeze(1).broadcast_to((P, NT, C)),
                                                   ALU.add).then_inc(resid_s, 1)
                            if nxt:
                                wait(pool, tok_in, (w + 1) * 16 + 16, begun)
                                wait(pool, resid_s, w + 1, begun)
                                wait(pool, xn_s, (w + 1) * NT, begun)
                                for n in range(NT):
                                    pool.indirect_dma_start(emb[:, n, :], None, dram["table"],
                                                            bass.IndirectOffsetOnAxis(ap=tok[:, n:n + 1], axis=0)).then_inc(emb_in, 16)
                        if t == 43 and nxt:
                            wait(pool, emb_in, (w + 2) * 16 * NT, begun)
                            pool.tensor_tensor(emb[:, :, :], emb[:, :, :], b_tok[:, :].unsqueeze(1).broadcast_to((P, NT, C)),
                                               ALU.add).then_inc(emb_b, 1)
                        if t == 49 and nxt:
                            wait(pool, x_turn, (w + 1) * 4, begun)
                            layer_norm(emb, mv1, var1_sb[:, :], rstd1, xn, stats1, var1, rstd1_s, xn_s, w + 1)
                        if t == 60 and prv:
                            wait(pool, x2_turn, (w - 1) * 4, begun)
                            wait(pool, sent, (w - 1) * 16 * 2 * NT, begun)
                            layer_norm(h2, mv2, var2_sb[:, :], rstd2, xn2, stats2, var2, rstd2_s, xn2_s, w - 1)
                        if t == RANK_AT + 5 and prv:
                            wait(pool, slots_s, w, begun)
                            pool.wait_ge(zeroed, 16 * G)
                            for n in range(NT):
                                for k in range(2):
                                    pool.indirect_dma_start(dram["slots"], bass.IndirectOffsetOnAxis(ap=slot_at[:, n, k:k + 1], axis=0),
                                                            xn2[:, n, :], None, bounds_check=SLOTS - 1, oob_is_err=False).then_inc(sent, 16)

                pool.wait_ge(consts, CONSTS)
                windows(pool, window)
                pool.wait_ge(zeroed, 16 * G)
                wait(pool, sent, NB * 16 * 2 * NT, begun)


            @block.scalar
            def _(act):
                def window(w, flags):
                    prv, cur, nxt = flags
                    for t in range(WIN):
                        g, o = t // STEPS, t % STEPS
                        if cur:
                            hp = t % 2
                            if hp == 0:
                                wait(act, av_s, w * (WIN // 2) + t // 2 - 1)
                            for i in range(2):
                                act.wait_ge(s2_s, (w * WIN + t) * 2 + i + 1)
                                act.activation(probs[(t // 2) % 2][:, 2 * hp + i, :], s2_ps[:, RING[2 * o + i], :], ACT.Exp,
                                               scale=HD ** -0.5).then_inc(exp_s, 1)
                        for at, lu, nh in ((18, g, 0), (2, g - 1, 1)):
                            if o == at and here(flags, lu):
                                u = w * G + lu
                                act.wait_ge(av_s, u * NT * 2 + nh * NT + NT)
                                wait(act, o_turn, (u - 1) * 2 + nh + 1)
                                act.activation(oT[:, nh, :], o_ps[:, :], ACT.Copy).then_inc(oT_s, 1)
                        work = small_work(t - 1)
                        if work is None or not here(flags, work[1]):
                            continue
                        name, lu, part = work
                        u, b, gb = w * G + lu, w + lu // G, lu % G
                        b_before, g_before = w + (lu - 1) // G, (lu - 1) % G
                        if name == "qk":
                            cols = slice(512 * part, 512 * part + 512)
                            act.wait_ge(qk_s, u * 2 + part + 1)
                            wait(act, split_s, (u - 1) * 2 + part + 1)
                            act.activation(qk_full[:, cols], m_ps[:, :], ACT.Identity, bias=b_qk[:, gb:gb + 1]).then_inc(qk_fulls, 1)
                            wait(act, stack_in[g_before], (b_before + 1) * 192)
                            act.activation(qk_part[0][:, cols], m_ps[:, :], ACT.Identity, bias=b_qk[:, gb:gb + 1]).then_inc(qk_out, 1)
                        elif name == "max_turn":
                            act.wait_ge(max_turn, u + 1)
                            wait(act, max_in[g_before], (b_before + 1) * 16)
                            act.activation(max_rows[:, :], m_bf[0:3 * HG * NT, 0:P], ACT.Copy).then_inc(max_rows_s, 1)
                        elif name in ("x_turn", "on_turn", "x2_turn"):
                            came, went, dst, free, n = {
                                "x_turn": (x_turn, xT_s, xnT, v_turn, b * G),
                                "on_turn": (on_turn, onT_s, turned, gate_mm, b),
                                "x2_turn": (x2_turn, x2T_s, turned, out_mm, b * 4 + 4),
                            }[name]
                            act.wait_ge(came, b * 4 + part + 1)
                            wait(act, free, n)
                            act.activation(dst[:, :, 2 * P * part:2 * P * part + 2 * P],
                                           m_ps[:, :].rearrange("p (c n) -> p c n", c=CC), ACT.Copy).then_inc(went, 1)
                        elif name == "gate":
                            act.wait_ge(gate_mm, b + 1)
                            wait(act, route, b * ROUTE1)
                            act.activation(gate_e[:, :, :].rearrange("p n e -> p (n e)"), m_ps[:, 0:NT * E_], ACT.Exp,
                                           scale=-1.0).then_inc(gate_s, 1)

                act.wait_ge(loads, 16 * 8)
                windows(act, window)

            @block.vector
            def _(dve):
                def then(ins, s, value):
                    ins.then_inc(s, 1)
                    dve.wait_ge(s, value)

                def statistics(src, stat, mv, stat_done, b, part):
                    for n in (2 * part, 2 * part + 1):
                        dve.bn_stats(stat[:, n, :], src[:, n, :]).then_inc(stat_done, 1)
                    wait(dve, stat_done, b * (2 * NT) + 4 * part + 2, begun)
                    for n in (2 * part, 2 * part + 1):
                        dve.bn_aggr(mv[:, n, :], stat[:, n, :]).then_inc(stat_done, 1)

                def choose_experts(b, at):
                    k = b * ROUTE1
                    k2 = k + 2 + 2 * NT
                    if at == 0:
                        dve.wait_ge(gate_s, b + 1)
                        then(dve.tensor_scalar(gate_p[:, :, :], gate_e[:, :, :], 1.0, None, ALU.add), route, k + 1)
                        dve.reciprocal(gate_p[:, :, :], gate_p[:, :, :]).then_inc(route, 1)
                    elif at in (1, 2, 3, 4):
                        wait(dve, route, k + 2, begun)
                        for n in (2 * at - 2, 2 * at - 1):
                            dve.max(top8[:, n, :], gate_p[:, n, :]).then_inc(route, 1)
                    elif at in (5, 6, 7, 8):
                        wait(dve, route, k + 2 + NT, begun)
                        for n in (2 * at - 10, 2 * at - 9):
                            dve.max_index(top8_at[:, n, :], top8[:, n, :], gate_p[:, n, :]).then_inc(route, 1)
                    elif at == 9:
                        dve.wait_ge(route, k2)
                        then(dve.tensor_tensor(gsum[:, :], top8[:, :, 0], top8[:, :, 1], ALU.add), route, k2 + 1)
                        dve.tensor_scalar(gsum[:, :], gsum[:, :], 1e-6, None, ALU.add).then_inc(route, 1)
                    elif at == 10:
                        dve.wait_ge(route, k2 + 2)
                        then(dve.reciprocal(gsum[:, :], gsum[:, :]), route, k2 + 3)
                        dve.tensor_tensor(weight2[:, :, :], top8[:, :, 0:2], gsum[:, :].unsqueeze(2).broadcast_to((P, NT, 2)),
                                          ALU.mult).then_inc(route, 1)
                        dve.tensor_copy(sel[:, :, :], top8_at[:, :, 0:2]).then_inc(route, 1)
                    elif at == 11:
                        dve.wait_ge(route, k2 + 5)
                        for i in range(2):
                            dve.tensor_tensor(hot[i][:, :, :], expert_iota[:, :].unsqueeze(1).broadcast_to((P, NT, E_)),
                                              sel[:, :, i:i + 1].broadcast_to((P, NT, E_)), ALU.is_equal).then_inc(route, 1)
                    elif at == 12:
                        dve.wait_ge(route, k2 + 7)
                        wait(dve, rank_mm, b)
                        dve.tensor_tensor(hot_bf[:, :, :], hot[0][:, :, :], hot[1][:, :, :], ALU.add).then_inc(route, 1)

                def give_slots(b, at):
                    k = b * ROUTE2
                    if at == 0:
                        dve.wait_ge(rank_mm, b + 1)
                        ranks = m_ps[:, 0:NT * E_].rearrange("p (n e) -> p n e", n=NT)
                        for i in range(2):
                            dve.tensor_tensor(picked[i][:, :, :], ranks, hot[i][:, :, :], ALU.mult).then_inc(picked_s, 1)
                    elif at == 1:
                        dve.wait_ge(picked_s, b * 2 + 2)
                        for i in range(2):
                            dve.tensor_reduce(rank[:, :, i], picked[i][:, :, :], AX.X, ALU.add).then_inc(route2, 1)
                        dve.tensor_reduce(hot_sum[:, :], hot_bf[:, :, :].rearrange("p n e -> p e n"), AX.X, ALU.add).then_inc(route2, 1)
                    elif at == 2:
                        dve.wait_ge(route2, k + 3)
                        dve.tensor_tensor(carry_bf[:, :], carry_bf[:, :], hot_sum[:, :], ALU.add).then_inc(route2, 1)
                        dve.tensor_scalar(valid[:, :, :], rank[:, :, :], float(CAP), None, ALU.is_lt).then_inc(route2, 1)
                        dve.scalar_tensor_tensor(slot[:, :, :], sel[:, :, :], float(CAP), rank[:, :, :], ALU.mult, ALU.add).then_inc(route2, 1)
                    elif at == 3:
                        dve.wait_ge(route2, k + 6)
                        then(dve.scalar_tensor_tensor(slot[:, :, :], slot[:, :, :], float(SLOTS), valid[:, :, :], ALU.subtract, ALU.mult), route2, k + 7)
                        wait(dve, sent, b * 16 * 2 * NT)
                        dve.tensor_scalar(slot_at[:, :, :], slot[:, :, :], float(SLOTS), None, ALU.add).then_inc(slots_s, 1)
                    elif at == 4:
                        cols = bass.ds(b * 2 * NT, 2 * NT)
                        dve.tensor_scalar(slot_of[:, cols], slot[:, :, :].rearrange("p n k -> p (n k)"), float(SLOTS), float(SLOTS - 1), ALU.add, ALU.min)
                        dve.tensor_tensor(weight_of[:, cols], weight2[:, :, :].rearrange("p n k -> p (n k)"),
                                          valid[:, :, :].rearrange("p n k -> p (n k)"), ALU.mult).then_inc(route2, 1)
                        dve.wait_ge(route2, k + 8)

                def window(w, flags):
                    prv, cur, nxt = flags
                    for t in range(WIN):
                        g, o = t // STEPS, t % STEPS
                        ahead = t + LEAD
                        lu, step = ahead // STEPS, ahead % STEPS
                        if here(flags, lu):
                            u = w * G + lu
                            if step == 0:
                                wait(dve, neg_s, (u - 1) * 5 + 1)
                            for half in range(2):
                                dve.wait_ge(s1_s, u * 64 + step * 2 + half + 1)
                                dve.tensor_reduce(half_max[:, step, half:half + 1], s1_ps[:, RING[2 * step + half], :], AX.X, ALU.max).then_inc(s1_max, 1)
                            if step == STEPS - 1:
                                k = u * 5
                                dve.wait_ge(s1_max, u * 64 + 64)
                                then(dve.tensor_reduce(neg_max[:, :], half_max[:, :, :], AX.X, ALU.max, negate=True), neg_s, k + 1)
                                wait(dve, max_turn, u)
                                then(dve.tensor_copy(neg_part[:, 0, :], neg_max[:, :]), neg_s, k + 2)
                                then(dve.tensor_tensor(neg_rest[:, :], neg_max[:, :], neg_part[:, 0, :], ALU.subtract), neg_s, k + 3)
                                then(dve.tensor_copy(neg_part[:, 1, :], neg_rest[:, :]), neg_s, k + 4)
                                dve.tensor_tensor(neg_part[:, 2, :], neg_rest[:, :], neg_part[:, 1, :], ALU.subtract).then_inc(neg_s, 1)
                        if t - 2 in OP_AT and prv:
                            part = OP_AT.index(t - 2)
                            dve.wait_ge(h2_s, (w - 1) * 4 + part + 1)
                            if part == 0:
                                wait(dve, xn2_s, (w - 1) * NT)
                            statistics(h2, stat2, mv2, stats2, w - 1, part)
                        if 46 <= t < 50 and nxt:
                            dve.wait_ge(emb_b, w + 2)
                            if t == 46:
                                wait(dve, xn_s, (w + 1) * NT)
                            statistics(emb, stat1, mv1, stats1, w + 1, t - 46)
                        if GATE_AT + 1 < t <= GATE_AT + 14 and prv:
                            choose_experts(w - 1, t - GATE_AT - 2)
                        if RANK_AT + 1 < t <= RANK_AT + 5 and prv:
                            give_slots(w - 1, t - RANK_AT - 1)
                        work = small_work(t - 1)
                        if work is None or not here(flags, work[1]):
                            continue
                        name, lu, part = work
                        u, b, gb = w * G + lu, w + lu // G, lu % G
                        if name == "o_turn":
                            dve.wait_ge(o_turn, u * 2 + part + 1)
                            heads = m_ps[:, :].rearrange("p (n h d) -> p n h d", n=4, h=HG)
                            sums = rsum[:, part, :].rearrange("p (n h) -> p n h", n=4)
                            then(dve.reciprocal(sums, heads[:, :, :, HD]), rsum_s, u * 2 + part + 1)
                            if gb == 0:
                                wait(dve, on_turn, b * 4)
                            dst = o_n[:, 4 * part:4 * part + 4, 64 * gb:64 * gb + 64].rearrange("p n (h d) -> p n h d", h=HG)
                            dve.tensor_tensor(dst, heads[:, :, :, 0:HD], sums.unsqueeze(3).broadcast_to((P, 4, HG, HD)), ALU.mult).then_inc(on_s, 1)
                        elif name == "v":
                            dve.wait_ge(v_turn, u + 1)
                            wait(dve, av_s, (u - G) * 2 * NT + 2 * NT)
                            bias = b_v[:, 64 * gb:64 * gb + 64].rearrange("p (h d) -> p h d", h=HG).unsqueeze(1).broadcast_to((P, NT, HG, HD))
                            dve.tensor_tensor(v_sb[gb][:, :, :, 0:HD], m_ps[:, :].rearrange("p (n h d) -> p n h d", n=NT, h=HG), bias,
                                              ALU.add).then_inc(v_s, 1)
                        elif name == "out":
                            dve.wait_ge(out_mm, b * 4 + part + 1)
                            dve.wait_ge(resid_s, b + 1)
                            if part == 0:
                                wait(dve, h2_st, b * 16)
                                wait(dve, xn2_s, b * NT)
                            dve.tensor_tensor(h2[:, 2 * part:2 * part + 2, :], m_ps[:, :].rearrange("p (n c) -> p n c", n=2),
                                              resid[:, 2 * part:2 * part + 2, :], ALU.add).then_inc(h2_s, 1)
                        elif name == "rank":
                            give_slots(b, 0)

                dve.wait_ge(consts, CONSTS)
                dve.wait_ge(loads, 16 * 8)
                windows(dve, window)

            @block.tensor
            def _(pe):
                def turn4(src, part, done):
                    for c in range(CC):
                        for n in range(2):
                            last = pe.transpose(m_ps[:, (2 * c + n) * P:(2 * c + n + 1) * P],
                                                src[:, 2 * part + n, c * P:(c + 1) * P], ident[:, :])
                    last.then_inc(done, 1)

                def do_small(work, w):
                    name, lu, part = work
                    u, b, gb = w * G + lu, w + lu // G, lu % G
                    if name == "o_turn":
                        pe.wait_ge(oT_s, u * 2 + part + 1)
                        for n in range(4):
                            last = pe.transpose(m_ps[:, n * P:(n + 1) * P], oT[:, part, n * P:(n + 1) * P], ident[:, :])
                        last.then_inc(o_turn, 1)
                    elif name == "qk":
                        if part == 0:
                            pe.wait_ge(xT_s, b * 4 + 4)
                        for c in range(CC):
                            last = pe.matmul(m_ps[:, :], wqk[:, c, gb, :], xnT[:, c, 512 * part:512 * part + 512],
                                             start=(c == 0), stop=(c == CC - 1))
                        last.then_inc(qk_s, 1)
                    elif name == "v":
                        for n in range(NT):
                            for c in range(CC):
                                last = pe.matmul(m_ps[:, 64 * n:64 * n + 64], xnT[:, c, P * n:P * n + P], wv[:, c, 64 * gb:64 * gb + 64],
                                                 start=(c == 0), stop=(c == CC - 1))
                        last.then_inc(v_turn, 1)
                    elif name == "max_turn":
                        pe.wait_ge(neg_s, u * 5 + 5)
                        pe.transpose(m_bf[0:3 * HG * NT, 0:P], neg_part[:, :, :].rearrange("p a n -> p (a n)"), ident_bf[:, :]).then_inc(max_turn, 1)
                    elif name == "on_turn":
                        pe.wait_ge(on_s, b * G * 2 + G * 2)
                        turn4(o_n, part, on_turn)
                    elif name == "x_turn":
                        pe.wait_ge(xn_s, b * NT + 2 * part + 2)
                        turn4(xn, part, x_turn)
                    elif name == "x2_turn":
                        pe.wait_ge(xn2_s, b * NT + 2 * part + 2)
                        turn4(xn2, part, x2_turn)
                    elif name == "out":
                        pe.wait_ge(onT_s, b * 4 + part + 1)
                        for n in range(2):
                            at = (2 * part + n) * P
                            for c in range(CC):
                                last = pe.matmul(m_ps[:, C * n:C * n + C], turned[:, c, at:at + P], wo[:, c, :],
                                                 start=(c == 0), stop=(c == CC - 1))
                        last.then_inc(out_mm, 1)
                    elif name == "gate":
                        pe.wait_ge(x2T_s, b * 4 + 4)
                        for n in range(NT):
                            for c in range(CC):
                                last = pe.matmul(m_ps[:, E_ * n:E_ * n + E_], turned[:, c, P * n:P * n + P], gw[:, c, :],
                                                 start=(c == 0), stop=(c == CC - 1))
                        last.then_inc(gate_mm, 1)
                    elif name == "rank":
                        pe.wait_ge(route, b * ROUTE1 + ROUTE1)
                        wait(pe, route2, b * ROUTE2)
                        flat = hot_bf[:, :, :].rearrange("p n e -> p (n e)")
                        pe.matmul(m_ps[:, 0:NT * E_], before_bf[:, :], flat, start=True, stop=False)
                        for n in range(1, NT):
                            pe.matmul(m_ps[:, n * E_:NT * E_], ones_bf[:, :], flat[:, 0:(NT - n) * E_], start=False, stop=False)
                        pe.matmul(m_ps[:, 0:NT * E_], ones_bf[:, :], carry_bf[:, :].unsqueeze(1).broadcast_to((P, NT, E_)),
                                  start=False, stop=True).then_inc(rank_mm, 1)

                def window(w, flags):
                    prv, cur, nxt = flags
                    before = ("max_turn", 0, 0) if cur else ("o_turn", -1, 0) if prv else None
                    for t in range(WIN):
                        ahead = t + LEAD
                        lu, step = ahead // STEPS, ahead % STEPS
                        g, o = t // STEPS, t % STEPS
                        nh, mt, hp = o // 16, (o % 16) // 2, o % 2
                        if here(flags, lu) and step == 0:
                            pe.wait_ge(stack_in[lu % G], (w + lu // G + 1) * 192)
                        if cur and o == 0:
                            pe.wait_ge(max_in[g], (w + 1) * 16)
                        for i in range(2):
                            if here(flags, lu):
                                u, gb = w * G + lu, lu % G
                                hh, n = step // NT, step % NT
                                wait(pe, s1_max, (w + 3) * (G * SC) + ((lu - 3 * G) * SC + bank_user_before(2 * step + i) + 1))
                                pe.matmul(s1_ps[:, RING[2 * step + i], :], q_stack[gb][0:KQ, hh * N + n * P:hh * N + n * P + P],
                                          k_stack[gb][0:KQ, hh * N + i * 512:hh * N + i * 512 + 512],
                                          start=True, stop=True).then_inc(s1_s, 1)
                            if cur:
                                hh = 2 * hp + i
                                wait(pe, exp_s, (w * G + g) * SC + bank_user_before(2 * o + i) + 1)
                                pe.matmul(s2_ps[:, RING[2 * o + i], :], k_stack[g][0:KS, hh * N + mt * P:hh * N + mt * P + P],
                                          q_stack[g][0:KS, hh * N + nh * 512:hh * N + nh * 512 + 512],
                                          start=True, stop=True).then_inc(s2_s, 1)
                        lp = (t - 1) // 2 - 1
                        if t % 2 == 1 and (cur if lp >= 0 else prv):
                            q = w * (WIN // 2) + lp
                            g, mt = (lp // 16) % G, lp % NT
                            pe.wait_ge(exp_s, q * 4 + 4)
                            if lp % 16 == 0:
                                pe.wait_ge(v_s, w * G + g + 1)
                            if mt == 0:
                                wait(pe, oT_s, w * (2 * G) + lp // NT)
                            for hh in range(HG):
                                last = pe.matmul(o_ps[32 * hh:32 * hh + 32, :], v_sb[g][:, mt, hh, :], probs[lp % 2][:, hh, :],
                                                 start=(mt == 0), stop=(mt == NT - 1))
                            last.then_inc(av_s, 1)
                        work = small_work(t)
                        if work is not None and here(flags, work[1]):
                            if before is not None:
                                wait(pe, *taken(before, w))
                            do_small(work, w)
                            before = work

                pe.wait_ge(consts, CONSTS)
                pe.wait_ge(loads, 16 * 8)
                windows(pe, window)


def experts(nc, begun, dram, CAP):
    TE = 5
    ST = CAP // TE
    SB = ST // P
    YB = (SB + 1) // 2
    PAIRS = E_ // 2
    NI = E_ * TE
    HI, LO = 0, 1
    PARTS = ((HI, HI), (HI, LO), (LO, HI))
    assert ST * TE == CAP and SB * P == ST and ST <= 512
    ctx = ExitStack()
    with ctx:
        def sb(name, shape, dt=F32):
            return ctx.enter_context(nc.sbuf_tensor(name, shape, dt))

        def sem(name):
            return ctx.enter_context(nc.semaphore(name))

        ident = sb("x_ident", [P, P])
        w1_raw = sb("w1_raw", [P, CC, F])
        w2_raw = sb("w2_raw", [P, FC, C])
        w1 = [[sb(f"w1_{e}_{h}", [P, CC, F], F32R) for h in range(2)] for e in range(2)]
        w2 = [[sb(f"w2_{e}_{h}", [P, FC, C], F32R) for h in range(2)] for e in range(2)]
        rows = [sb(f"rows{i}", [P, SB, C]) for i in range(2)]
        rowsT = [[sb(f"rowsT{i}_{h}", [P, CC, ST], F32R) for h in range(2)] for i in range(2)]
        hid_full = [sb(f"hid_full{i}", [P, FC, ST]) for i in range(2)]
        hid = [[sb(f"hid{i}_{h}", [P, FC, ST], F32R) for h in range(2)] for i in range(2)]
        y = [sb(f"y{i}", [P, SB, C]) for i in range(2)]
        turn_ps = ctx.enter_context(nc.psum_tensor("turn_ps", [P, CC, 512], F32))
        hid_ps = ctx.enter_context(nc.psum_tensor("hid_ps", [P, FC, 512], F32))
        y_ps = ctx.enter_context(nc.psum_tensor("y_ps", [P, 2, 512], F32))

        mask = sem("x_mask")
        w_in = sem("w_in")
        w_hi = sem("w_hi")
        w_lo = sem("w_lo")
        rows_in = [sem(f"rows_in{i}") for i in range(2)]
        turn_mm = sem("turn_mm")
        rowsT_hi = sem("rowsT_hi")
        rowsT_lo = sem("rowsT_lo")
        hid_mm = sem("hid_mm")
        gelu_s = sem("gelu_s")
        hid_lo = sem("hid_lo")
        y_mm = sem("y_mm")
        y_s = sem("y_s")
        y_st = [sem(f"y_st{i}") for i in range(2)]

        def pairs(eng, body):
            body(0, True, False)
            with eng.Fori(1, PAIRS - 1) as j:
                body(j, False, False)
            body(PAIRS - 1, False, True)

        with nc.Block() as block:

            @block.gpsimd
            def _(pool):
                pool.memset(ident[:, :], 0.0).then_inc(mask, 1)
                pool.wait_ge(mask, 1)
                pool.affine_select(out=ident[:, :], in_=ident[:, :], compare_op=ALU.not_equal, fill=1.0, base=0,
                                   pattern=[[-1, P]], channel_multiplier=1).then_inc(mask, 1)

            @block.sync
            def _(sp):
                def load_rows(i, par):
                    sp.dma_start(rows[par][:, :, :], dram["slots_t"][i]).then_inc(rows_in[par], 16)

                def load_w(e):
                    sp.dma_start(w1_raw[:, :, :], dram["w1"][e]).then_inc(w_in, 16)
                    sp.dma_start(w2_raw[:, :, :], dram["w2"][e]).then_inc(w_in, 16)

                load_rows(0, 0)
                load_w(0)
                load_rows(1, 1)

                def body(j, first, last):
                    for k in range(2 * TE):
                        i = j * (2 * TE) + k
                        if not (last and k >= 2 * TE - 2):
                            wait(sp, turn_mm, i + 1, begun)
                            load_rows(i + 2, k % 2)
                        if k % TE == 0 and not (last and k > 0):
                            wait(sp, w_lo, j * 4 + 2 * (k // TE) + 2, begun)
                            load_w(j * 2 + k // TE + 1)
                        wait(sp, y_s, i * YB + YB, begun)
                        sp.dma_start(dram["outs_t"][i], y[k % 2][:, :, :]).then_inc(y_st[k % 2], 16)

                pairs(sp, body)
                for par in range(2):
                    wait(sp, y_st[par], 16 * NI // 2, begun)

            @block.scalar
            def _(act):
                def turned_high(i, par):
                    act.wait_ge(turn_mm, i + 1)
                    wait(act, hid_mm, (i - 1) * FC)
                    act.activation(rowsT[par][HI][:, :, :], turn_ps[:, :, 0:ST], ACT.Copy).then_inc(rowsT_hi, 1)

                def body(j, first, last):
                    for k in range(2 * TE):
                        i = j * (2 * TE) + k
                        wait(act, y_mm, (i - 1) * YB)
                        for f in range(FC):
                            act.wait_ge(hid_mm, i * FC + f + 1)
                            act.activation(hid_full[k % 2][:, f, :], hid_ps[:, f, 0:ST], ACT.Gelu).then_inc(gelu_s, 1)
                            act.activation(hid[k % 2][HI][:, f, :], hid_ps[:, f, 0:ST], ACT.Gelu).then_inc(gelu_s, 1)
                        if not (last and k == 2 * TE - 1):
                            turned_high(i + 1, (k + 1) % 2)

                turned_high(0, 0)
                pairs(act, body)

            @block.vector
            def _(dve):
                def split_weights(e, par):
                    dve.wait_ge(w_in, e * 32 + 32)
                    wait(dve, y_mm, (e - 1) * TE * YB)
                    for raw, w in ((w1_raw, w1[par]), (w2_raw, w2[par])):
                        dve.tensor_copy(w[HI][:, :, :], raw[:, :, :]).then_inc(w_hi, 1)
                    for n, (raw, w) in enumerate(((w1_raw, w1[par]), (w2_raw, w2[par]))):
                        dve.wait_ge(w_hi, e * 2 + n + 1)
                        dve.tensor_tensor(w[LO][:, :, :], raw[:, :, :], w[HI][:, :, :].bitcast(F32), ALU.subtract).then_inc(w_lo, 1)

                def turned_low(i, par):
                    dve.wait_ge(rowsT_hi, i + 1)
                    wait(dve, hid_mm, (i - 1) * FC)
                    dve.tensor_tensor(rowsT[par][LO][:, :, :], turn_ps[:, :, 0:ST], rowsT[par][HI][:, :, :].bitcast(F32),
                                      ALU.subtract).then_inc(rowsT_lo, 1)

                def copy_out(i, par, stored):
                    wait(dve, y_st[par], stored * 16)
                    for q in range(YB):
                        n = min(2, SB - 2 * q)
                        dve.wait_ge(y_mm, i * YB + q + 1)
                        dve.tensor_copy(y[par][:, 2 * q:2 * q + n, :],
                                        y_ps[:, q, 0:n * C].rearrange("p (n c) -> p n c", n=n)).then_inc(y_s, 1)

                def body(j, first, last):
                    for k in range(2 * TE):
                        i = j * (2 * TE) + k
                        wait(dve, y_mm, (i - 1) * YB)
                        for f in range(FC):
                            dve.wait_ge(gelu_s, i * (2 * FC) + 2 * f + 2)
                            dve.tensor_tensor(hid[k % 2][LO][:, f, :], hid_full[k % 2][:, f, :], hid[k % 2][HI][:, f, :].bitcast(F32),
                                              ALU.subtract).then_inc(hid_lo, 1)
                        if not (last and k == 2 * TE - 1):
                            turned_low(i + 1, (k + 1) % 2)
                        if not (first and k == 0):
                            copy_out(i - 1, (k - 1) % 2, j * TE + (k + 1) // 2 - 1)
                        if k % TE == 2 and not (last and k > TE):
                            split_weights(j * 2 + k // TE + 1, (k // TE + 1) % 2)

                split_weights(0, 0)
                turned_low(0, 0)
                pairs(dve, body)
                copy_out(NI - 1, 1, NI // 2 - 1)

            @block.tensor
            def _(pe):
                def turn(i, par, nth):
                    pe.wait_ge(rows_in[par], nth * 16)
                    wait(pe, rowsT_lo, i)
                    for c in range(CC):
                        for n in range(SB):
                            last = pe.transpose(turn_ps[:, c, n * P:(n + 1) * P], rows[par][:, n, c * P:(c + 1) * P], ident[:, :])
                    last.then_inc(turn_mm, 1)

                def first_product(i, par, e_par):
                    pe.wait_ge(rowsT_lo, i + 1)
                    for f in range(FC):
                        wait(pe, gelu_s, (i - 1) * (2 * FC) + 2 * f + 2)
                        terms = [(c, a, b) for c in range(CC) for a, b in PARTS]
                        for c, a, b in terms:
                            last = pe.matmul(hid_ps[:, f, 0:ST], w1[e_par][a][:, c, f * P:(f + 1) * P], rowsT[par][b][:, c, :],
                                             start=((c, a, b) == terms[0]), stop=((c, a, b) == terms[-1]))
                        last.then_inc(hid_mm, 1)

                def second_product(i, par, e_par):
                    pe.wait_ge(hid_lo, i * FC + FC)
                    for q in range(YB):
                        wait(pe, y_s, (i - 1) * YB + q + 1)
                        for n in range(2 * q, min(2 * q + 2, SB)):
                            terms = [(f, a, b) for f in range(FC) for a, b in PARTS]
                            for f, a, b in terms:
                                last = pe.matmul(y_ps[:, q, (n % 2) * C:(n % 2) * C + C], hid[par][a][:, f, n * P:(n + 1) * P],
                                                 w2[e_par][b][:, f, :], start=((f, a, b) == terms[0]), stop=((f, a, b) == terms[-1]))
                        last.then_inc(y_mm, 1)

                def body(j, first, last):
                    for k in range(2 * TE):
                        i = j * (2 * TE) + k
                        if k % TE == 0:
                            pe.wait_ge(w_lo, j * 4 + 2 * (k // TE) + 2)
                        first_product(i, k % 2, k // TE)
                        if not (last and k == 2 * TE - 1):
                            nth = j * TE + (k + 1) // 2 + 1
                            turn(i + 1, (k + 1) % 2, nth)
                        if not (first and k == 0):
                            second_product(i - 1, (k - 1) % 2, ((k - 1) // TE) % 2)

                pe.wait_ge(mask, 2)
                turn(0, 0, 1)
                pairs(pe, body)
                second_product(NI - 1, 1, 1)


def combine(nc, begun, slot_of, weight_of, dram, NB):
    H = 2
    T = NT // H
    ctx = ExitStack()
    with ctx:
        def sb(name, shape, dt=F32):
            return ctx.enter_context(nc.sbuf_tensor(name, shape, dt))

        def sem(name):
            return ctx.enter_context(nc.semaphore(name))

        at = [sb(f"at{h}", [P, T * 2], I32) for h in range(H)]
        got = [sb(f"got{h}", [P, T, 2, C]) for h in range(H)]
        acc = [sb(f"acc{h}", [P, T, C]) for h in range(H)]
        at_s = sem("at_s")
        got_in = [sem(f"got_in{h}") for h in range(H)]
        acc_in = [sem(f"acc_in{h}") for h in range(H)]
        one_s = sem("one_s")
        acc_s = sem("acc_s")
        out_st = [sem(f"out_st{h}") for h in range(H)]

        def rows(eng, body):
            body(0)
            with eng.Fori(1, NB) as b:
                body(b)

        with nc.Block() as block:

            @block.sync
            def _(sp):
                def load(b):
                    for h in range(H):
                        wait(sp, out_st[h], b * 16, begun)
                        sp.dma_start(acc[h][:, :, :], dram["h2"][b][:, h * T:(h + 1) * T, :]).then_inc(acc_in[h], 16)

                rows(sp, load)

            @block.gpsimd
            def _(pool):
                def fetch(b):
                    for h in range(H):
                        wait(pool, got_in[h], b * 16 * 2 * T, begun)
                        cols = bass.ds(b * (2 * NT) + h * 2 * T, 2 * T)
                        pool.tensor_copy(at[h][:, :], slot_of[:, cols]).then_inc(at_s, 1)
                        wait(pool, at_s, b * H + h + 1, begun)
                        wait(pool, acc_s, (b * H + h - H + 1) * T, begun)
                        for n in range(T):
                            for k in range(2):
                                i = 2 * n + k
                                pool.indirect_dma_start(got[h][:, n, k, :], None, dram["outs"],
                                                        bass.IndirectOffsetOnAxis(ap=at[h][:, i:i + 1], axis=0)).then_inc(got_in[h], 16)

                rows(pool, fetch)

            @block.vector
            def _(dve):
                def add(b):
                    for h in range(H):
                        dve.wait_ge(got_in[h], (b + 1) * 16 * 2 * T)
                        dve.wait_ge(acc_in[h], (b + 1) * 16)
                        for k, done in ((0, one_s), (1, acc_s)):
                            for n in range(T):
                                col = b * (2 * NT) + (h * T + n) * 2 + k
                                dve.scalar_tensor_tensor(acc[h][:, n, :], got[h][:, n, k, :], weight_of[:, bass.ds(col, 1)], acc[h][:, n, :],
                                                         ALU.mult, ALU.add).then_inc(done, 1)
                            if k == 0:
                                dve.wait_ge(one_s, (b * H + h + 1) * T)

                rows(dve, add)

            @block.scalar
            def _(act):
                def store(b):
                    for h in range(H):
                        act.wait_ge(acc_s, (b * H + h + 1) * T)
                        act.dma_start(dram["out"][b][:, h * T:(h + 1) * T, :], acc[h][:, :, :]).then_inc(out_st[h], 16)

                rows(act, store)
                for h in range(H):
                    act.wait_ge(out_st[h], NB * 16)


def lm_tower(nc, a, NB):
    CAP = int(1.25 * NB * N * 2 / E_)
    SLOTS = E_ * CAP
    ST = CAP // 5
    h2 = nc.dram_tensor("h2_rows", (NB * N, C), F32).ap()
    slots = nc.dram_tensor("slot_rows", (SLOTS, C), F32).ap()
    outs = nc.dram_tensor("expert_rows", (SLOTS, C), F32).ap()
    by_row = lambda x: x.rearrange("(b n p) c -> b p n c", p=P, n=NT)
    dram = {
        "table": a["table"], "tok": a["tok"],
        "wqk": a["wqk"], "wv": a["wv"], "wo": a["wo"], "gw": a["gate"],
        "b_qk": a["b_qk"], "b_v": a["b_v"], "b_o": a["b_o"], "b_tok": a["b_tok"],
        "w1": a["w1"].rearrange("e (c p) f -> e p c f", p=P), "w2": a["w2"].rearrange("e (c p) d -> e p c d", p=P),
        "h2": by_row(h2), "out": by_row(a["out"]), "slots": slots, "outs": outs,
        "slots_t": slots.rearrange("(i n p) c -> i p n c", p=P, n=ST // P),
        "outs_t": outs.rearrange("(i n p) c -> i p n c", p=P, n=ST // P),
    }
    with ExitStack() as ctx:
        begun = ctx.enter_context(nc.semaphore("begun"))
        slot_of = ctx.enter_context(nc.sbuf_tensor("slot_of", [P, NB * 2 * NT], I32))
        weight_of = ctx.enter_context(nc.sbuf_tensor("weight_of", [P, NB * 2 * NT], F32))
        attention_and_routing(nc, begun, slot_of, weight_of, dram, NB, CAP)
        experts(nc, begun, dram, CAP)
        combine(nc, begun, slot_of, weight_of, dram, NB)


def lay_out(x, L0_tok_weight, L0_tok_bias, L0_attn_w_qkv, L0_attn_b_qkv, L0_attn_w_out, L0_attn_b_out,
            L0_ffn_gate_w, L0_ffn_w1, L0_ffn_w2):
    import numpy as np

    arr = lambda v: np.ascontiguousarray(np.asarray(v))
    by_chunk = lambda w: arr(np.asarray(w).T.reshape(CC, P, -1).transpose(1, 0, 2))
    nb = x.shape[0]
    w, b = np.asarray(L0_attn_w_qkv), np.asarray(L0_attn_b_qkv)
    qk_rows = np.array([[s * C + (g * HG + h) * HD + d for s in range(2) for d in range(HD) for h in range(HG)] for g in range(G)])
    return {
        "tok": arr(np.asarray(x).reshape(nb, NT, P).transpose(0, 2, 1)),
        "table": arr(np.asarray(L0_tok_weight).T),
        "wqk": arr(w[qk_rows.reshape(-1)].T.reshape(CC, P, G, P).transpose(1, 0, 2, 3)),
        "wv": by_chunk(w[2 * C:3 * C]), "wo": by_chunk(L0_attn_w_out), "gate": by_chunk(L0_ffn_gate_w),
        "b_qk": arr(b[qk_rows].T), "b_v": arr(b[2 * C:3 * C]), "b_o": arr(L0_attn_b_out), "b_tok": arr(L0_tok_bias),
        "w1": arr(L0_ffn_w1), "w2": arr(L0_ffn_w2),
    }


def kernel(**inputs):
    import numpy as np
    import concourse.bacc as bacc
    from concourse.bass_utils import run_bass_kernel_spmd

    nb = inputs["x"].shape[0]
    arrays = lay_out(**inputs)
    nc = bacc.Bacc("TRN2", target_bir_lowering=False, num_devices=1)
    a = {name: nc.dram_tensor("in_" + name, v.shape, mybir.dt.from_np(v.dtype), kind="ExternalInput").ap() for name, v in arrays.items()}
    a["out"] = nc.dram_tensor("out_rows", (nb * N, C), F32, kind="ExternalOutput").ap()
    lm_tower(nc, a, nb)
    r = run_bass_kernel_spmd(nc, [{"in_" + name: v for name, v in arrays.items()}], core_ids=[0])
    return np.asarray(r.results[0]["out_rows"]).reshape(nb, N, C)
```

```python
from contextlib import ExitStack

import concourse.bass as bass
from concourse import mybir

P = 128
F32 = mybir.dt.float32
F32R = mybir.dt.float32r
BF16 = mybir.dt.bfloat16
I32 = mybir.dt.int32
U32 = mybir.dt.uint32
ALU = mybir.AluOpType
ACT = mybir.ActivationFunctionType
AX = mybir.AxisListType

EPS = 1e-5
HEADS = 16
HD = 16
G = 4
HG = HEADS // G
C = 256
CC = C // P
N = 1024
NT = N // P
E_ = 16
F = 512
FC = F // P
STEPS = 2 * NT * 2
WIN = G * STEPS
LEAD = 42
KQ = 6 * HD
KS = KQ + 3
Q_TERMS = (0, 0, 0, 1, 1, 2)
K_TERMS = (0, 1, 2, 0, 1, 0)
ROW = C + 2
TE = 5
SC = 2 * STEPS
RING = tuple(i % 3 for i in range(SC - 1)) + (1,)
BT_AT = (14, 16, 18, 20)
OP_AT = (25, 30, 33, 36)
XT_AT = (62, 64, 66, 68)
X2T_AT = (78, 80, 82, 84)
GATE_AT, RANK_AT = 89, 100
RESID_AT = OP_AT[-1] + 3
EMB_AT = 43
STAT1_AT = (50, 52, 54, 56)
LN1_AT, LN2_AT = 57, 60
STACK_AT, MAX_AT = 14, 28
O_AT = (18, 2)
SEND_AT = (108, 121)


def small_work(t):
    if t < 0:
        return None
    g, o = t // STEPS, t % STEPS
    if o == 6:
        return "o_turn", g - 1, 1
    if o in (8, 10):
        return "qk", g + 2, (o - 8) // 2
    if o == 12:
        return "v", g // 2 * 2 + 2, g % 2
    if o == 22:
        return "o_turn", g, 0
    if o == 27:
        return "max_turn", g + 1, 0
    for name, at, rel in (("on_turn", BT_AT, -1), ("out", OP_AT, -1), ("x_turn", XT_AT, 1), ("x2_turn", X2T_AT, -1)):
        if t in at:
            return name, 4 * rel, at.index(t)
    if t == GATE_AT:
        return "gate", -4, 0
    if t == RANK_AT:
        return "rank", -4, 0
    return None


def bank_user_before(i):
    return max(k for k in range(i - SC, i) if RING[k % SC] == RING[i])


def is_int(x):
    return isinstance(x, int)


def wait(eng, sem, value, begun=None):
    if not is_int(value) or value > 0:
        if begun is not None and not is_int(value):
            value = eng.to_reg(value)
            eng.wait_ge(begun, 1)
        eng.wait_ge(sem, value)


def attention_and_routing(nc, begun, dram, NB, CAP):
    SLOTS = E_ * CAP
    SB = CAP // TE // P
    ctx = ExitStack()
    with ctx:
        def sb(name, shape, dt=F32):
            return ctx.enter_context(nc.sbuf_tensor(name, shape, dt))

        def sem(name):
            return ctx.enter_context(nc.semaphore(name))

        ident = sb("ident", [P, P])
        ident_bf = sb("ident_bf", [P, P], BF16)
        before_bf = sb("before_bf", [P, P], BF16)
        ones_bf = sb("ones_bf", [P, P], BF16)
        expert_iota = sb("expert_iota", [P, E_])
        minus_half = sb("minus_half", [P, NT])
        empty = sb("empty", [P, SB, ROW])
        token = sb("token", [P, NT])
        wqk = sb("wqk", [P, CC, G, P])
        wv = sb("wv", [P, CC, C])
        wo = sb("wo", [P, CC, C])
        gw = sb("gw", [P, CC, E_])
        b_qk = sb("b_qk", [P, G])
        b_v = sb("b_v", [P, C])
        b_o = sb("b_o", [P, C])
        b_tok = sb("b_tok", [P, C])

        tok = sb("tok", [P, NT], I32)
        emb = sb("emb", [P, NT, C])
        stat1 = sb("stat1", [P, NT, 6])
        mv1 = sb("mv1", [P, NT, 2])
        rstd1 = sb("rstd1", [P, NT])
        xn = sb("xn", [P, NT, C])
        xnT = sb("xnT", [P, CC, N])
        qk_full = sb("qk_full", [P, N])
        qk_rest = sb("qk_rest", [P, N])
        qk_part = [sb(f"qk_part{i}", [P, N], BF16) for i in range(3)]
        q_stack = [sb(f"q_stack{g}", [KS, HG * N], BF16) for g in range(G)]
        k_stack = [sb(f"k_stack{g}", [KS, HG * N], BF16) for g in range(G)]
        v_sb = [sb(f"v_sb{g}", [P, NT, HG, 32]) for g in range(G)]
        half_max = sb("half_max", [P, HG * NT, 2])
        neg_max = sb("neg_max", [P, HG * NT])
        neg_rest = sb("neg_rest", [P, HG * NT])
        neg_part = sb("neg_part", [P, 3, HG * NT], BF16)
        max_rows = sb("max_rows", [3 * HG * NT, P], BF16)
        probs = [sb(f"probs{i}", [P, HG, 512]) for i in range(2)]
        oT = sb("oT", [P, 2, 512])
        rsum = sb("rsum", [P, 2, 4 * HG])
        o_n = sb("o_n", [P, NT, C])
        turned = sb("turned", [P, CC, N])
        resid = sb("resid", [P, NT, C])
        h2 = sb("h2", [P, NT, C])
        stat2 = sb("stat2", [P, NT, 6])
        mv2 = sb("mv2", [P, NT, 2])
        rstd2 = sb("rstd2", [P, NT])
        xn2 = sb("xn2", [P, NT, ROW])
        gate_e = sb("gate_e", [P, NT, E_])
        gate_p = sb("gate_p", [P, NT, E_])
        top8 = sb("top8", [P, NT, 8])
        top8_at = sb("top8_at", [P, NT, 8], U32)
        gsum = sb("gsum", [P, NT])
        weight2 = sb("weight2", [P, NT, 2])
        sel = sb("sel", [P, NT, 2])
        hot = [sb(f"hot{k}", [P, NT, E_]) for k in range(2)]
        hot_bf = sb("hot_bf", [P, NT, E_], BF16)
        carry_bf = sb("carry_bf", [P, E_], BF16)
        hot_sum = sb("hot_sum", [P, E_])
        picked = [sb(f"picked{k}", [P, NT, E_]) for k in range(2)]
        rank = sb("rank", [P, NT, 2])
        valid = sb("valid", [P, NT, 2])
        begun_mark = sb("begun_mark", [P, 1])
        slot = sb("slot", [P, NT, 2])
        slot_at = sb("slot_at", [P, NT, 2], I32)
        var1_sb = sb("var1_sb", [P, NT])
        var2_sb = sb("var2_sb", [P, NT])

        s2_ps = ctx.enter_context(nc.psum_tensor("s2_ps", [P, 3, 512], F32))
        s1_ps = ctx.enter_context(nc.psum_tensor("s1_ps", [P, 3, 512], F32))
        o_ps = ctx.enter_context(nc.psum_tensor("o_ps", [P, 512], F32))
        m_ps = ctx.enter_context(nc.psum_tensor("m_ps", [P, 512], F32))
        m_bf = m_ps[:, :].bitcast(BF16)

        consts = sem("consts")
        ones_s = sem("ones_s")
        loads = sem("loads")
        tok_in = sem("tok_in")
        emb_in = sem("emb_in")
        emb_b = sem("emb_b")
        stats1 = sem("stats1")
        var1 = sem("var1")
        rstd1_s = sem("rstd1_s")
        xn_s = sem("xn_s")
        x_turn = sem("x_turn")
        xT_s = sem("xT_s")
        qk_s = sem("qk_s")
        qk_fulls = sem("qk_fulls")
        qk_out = sem("qk_out")
        split_a = sem("split_a")
        split_b = sem("split_b")
        split_s = sem("split_s")
        stack_in = [sem(f"stack_in{g}") for g in range(G)]
        v_turn = sem("v_turn")
        v_s = sem("v_s")
        s1_s = sem("s1_s")
        s1_max = sem("s1_max")
        neg_s = sem("neg_s")
        max_turn = sem("max_turn")
        max_rows_s = sem("max_rows_s")
        max_in = [sem(f"max_in{g}") for g in range(G)]
        s2_s = sem("s2_s")
        exp_s = sem("exp_s")
        av_s = sem("av_s")
        oT_s = sem("oT_s")
        o_turn = sem("o_turn")
        rsum_s = sem("rsum_s")
        on_s = sem("on_s")
        on_turn = sem("on_turn")
        onT_s = sem("onT_s")
        resid_s = sem("resid_s")
        out_mm = sem("out_mm")
        h2_s = sem("h2_s")
        h2_st = sem("h2_st")
        stats2 = sem("stats2")
        var2 = sem("var2")
        rstd2_s = sem("rstd2_s")
        xn2_s = sem("xn2_s")
        x2_turn = sem("x2_turn")
        x2T_s = sem("x2T_s")
        gate_mm = sem("gate_mm")
        gate_s = sem("gate_s")
        route = sem("route")
        rank_mm = sem("rank_mm")
        picked_s = sem("picked_s")
        route2 = sem("route2")
        slots_s = sem("slots_s")
        sent = sem("sent")
        second_s = sem("second_s")
        zeroed = sem("zeroed")
        v_init = sem("v_init")
        ROUTE1, ROUTE2 = 26, 8
        LOADS = 8
        CONSTS = 12 + G

        def taken(work, w):
            name, lu, part = work
            u, b = w * G + lu, w + lu // G
            return {
                "o_turn": (on_s, u * 2 + part + 1), "qk": (qk_out, u * 2 + part + 1), "v": (v_s, (u + part + 1) * 2),
                "max_turn": (max_rows_s, u + 1), "on_turn": (onT_s, b * 4 + part + 1), "out": (h2_s, b * 4 + part + 1),
                "x_turn": (xT_s, b * 4 + part + 1), "x2_turn": (x2T_s, b * 4 + part + 1), "gate": (gate_s, b + 1),
                "rank": (picked_s, b * 2 + 2),
            }[name]

        def windows(eng, window):
            full = (True, True, True)
            flags = lambda w: (w >= 1, 0 <= w < NB, w + 1 < NB)
            window(-1, flags(-1))
            window(0, flags(0))
            if NB > 2:
                with eng.Fori(1, NB - 1) as w:
                    window(w, full)
            window(NB - 1, flags(NB - 1))
            window(NB, flags(NB))

        def here(flags, lu):
            return flags[lu // G + 1]

        with nc.Block() as block:

            @block.sync
            def _(sp):
                for dst, src in ((wqk, dram["wqk"]), (wv, dram["wv"]), (wo, dram["wo"]), (gw, dram["gw"]), (b_qk, dram["b_qk"])):
                    sp.dma_start(dst.ap(), src).then_inc(loads, 16)
                for dst, src in ((b_tok, dram["b_tok"]), (b_v, dram["b_v"]), (b_o, dram["b_o"])):
                    sp.dma_start(dst[:, :], src.rearrange("(a n) -> a n", a=1).broadcast_to((P, C))).then_inc(loads, 16)

                def window(w, flags):
                    prv, cur, nxt = flags
                    for t in range(WIN):
                        g, o = t // STEPS, t % STEPS
                        if t == 0 and nxt:
                            wait(sp, emb_in, (w + 1) * 16 * NT, begun)
                            sp.dma_start(tok[:, :], dram["tok"][w + 1]).then_inc(tok_in, 16)
                        if is_int(w) and w == 0 and o == 1:
                            if g == 0:
                                sp.wait_ge(consts, CONSTS)
                                sp.dma_start(dram["spare"], empty[:, :, 0:C]).then_inc(zeroed, 16)
                            rows = SLOTS // G
                            for n in range(SB):
                                sp.dma_start(
                                    dram["slots"][g * rows:(g + 1) * rows, :].rearrange("(r n p) c -> n p r c", p=P, n=SB)[n],
                                    empty[:, n, :].unsqueeze(1).broadcast_to((P, rows // (SB * P), ROW)),
                                ).then_inc(zeroed, 16)
                        if o == STACK_AT and here(flags, g + 2):
                            u, gb, b = w * G + g + 2, (g + 2) % G, w + (g + 2) // G
                            wait(sp, split_s, u * 2 + 2, begun)
                            wait(sp, s2_s, (u - G + 1) * SC, begun)
                            for n in range(6):
                                sp.dma_start(q_stack[gb][n * HD:(n + 1) * HD, :], qk_part[Q_TERMS[n]][0:64, :]).then_inc(stack_in[gb], 16)
                                sp.dma_start(k_stack[gb][n * HD:(n + 1) * HD, :], qk_part[K_TERMS[n]][64:128, :]).then_inc(stack_in[gb], 16)
                        if o == MAX_AT and here(flags, g + 1):
                            wait(sp, max_rows_s, w * G + g + 2, begun)
                            sp.dma_start(q_stack[(g + 1) % G][KQ:KS, :], max_rows[:, :]).then_inc(max_in[(g + 1) % G], 16)
                        if t == OP_AT[-1] + 2 and prv:
                            wait(sp, h2_s, w * 4, begun)
                            sp.dma_start(dram["out"][w - 1], h2[:, :, :]).then_inc(h2_st, 16)

                windows(sp, window)
                wait(sp, h2_st, 16 * NB, begun)

            @block.gpsimd
            def _(pool):
                pool.memset(begun_mark[:, :], 0.0).then_inc(begun, 1)
                pool.memset(ident[:, :], 0.0).then_inc(consts, 1)
                pool.memset(ident_bf[:, :], 0.0).then_inc(consts, 1)
                pool.memset(ones_bf[:, :], 1.0).then_inc(consts, 1)
                pool.memset(minus_half[:, :], -0.5).then_inc(consts, 1)
                pool.memset(empty[:, :, :], 0.0).then_inc(consts, 1)
                pool.memset(carry_bf[:, :], 0.0).then_inc(consts, 1)
                pool.iota(expert_iota[:, :], pattern=[[1, E_]], base=0, channel_multiplier=0,
                          allow_small_or_imprecise_dtypes=True).then_inc(consts, 1)
                pool.iota(token[:, :], pattern=[[P, NT]], base=0, channel_multiplier=1,
                          allow_small_or_imprecise_dtypes=True).then_inc(consts, 1)
                pool.wait_ge(consts, 8)
                pool.iota(empty[:, :, C], pattern=[[P, SB]], base=NB * N, channel_multiplier=1,
                          allow_small_or_imprecise_dtypes=True).then_inc(consts, 1)
                for m in (ident, ident_bf):
                    pool.affine_select(out=m[:, :], in_=m[:, :], compare_op=ALU.not_equal, fill=1.0, base=0,
                                       pattern=[[-1, P]], channel_multiplier=1).then_inc(consts, 1)
                pool.affine_select(out=before_bf[:, :], in_=ones_bf[:, :], compare_op=ALU.is_gt, fill=0.0, base=0,
                                   pattern=[[1, P]], channel_multiplier=-1).then_inc(consts, 1)
                for g in range(G):
                    pool.memset(v_sb[g][:, :, :, HD:32], 0.0).then_inc(v_init, 1)
                pool.wait_ge(v_init, G)
                for g in range(G):
                    pool.memset(v_sb[g][:, :, :, HD:HD + 1], 1.0).then_inc(consts, 1)
                pool.wait_ge(consts, CONSTS)
                pool.wait_ge(loads, 16 * LOADS)

                def layer_norm(src, mv, var, rstd, dst, stat_done, var_done, rstd_done, out_done, b, apply):
                    wait(pool, stat_done, b * (2 * NT) + 2 * NT, begun)
                    pool.tensor_scalar(var, mv[:, :, 1], EPS, None, ALU.add).then_inc(var_done, 1)
                    wait(pool, var_done, b + 1, begun)
                    pool.tensor_tensor(rstd[:, :], var, minus_half[:, :], ALU.pow).then_inc(rstd_done, 1)
                    if not apply:
                        return
                    wait(pool, rstd_done, b + 1, begun)
                    for n in range(NT):
                        pool.tensor_scalar(dst[:, n, 0:C], src[:, n, :], mv[:, n, 0:1], rstd[:, n:n + 1],
                                           ALU.subtract, ALU.mult).then_inc(out_done, 1)

                def window(w, flags):
                    prv, cur, nxt = flags
                    for t in range(WIN):
                        g, o = t // STEPS, t % STEPS
                        if o in (9, 11) and here(flags, g + 2):
                            half, u = (o - 9) // 2, w * G + g + 2
                            cols = slice(512 * half, 512 * half + 512)
                            wait(pool, qk_fulls, u * 2 + half + 1, begun)
                            wait(pool, qk_out, u * 2 + half + 1, begun)
                            pool.tensor_tensor(qk_rest[:, cols], qk_full[:, cols], qk_part[0][:, cols], ALU.subtract).then_inc(split_a, 1)
                            pool.tensor_tensor(qk_part[1][:, cols], qk_full[:, cols], qk_part[0][:, cols], ALU.subtract).then_inc(split_b, 1)
                            wait(pool, split_a, u * 2 + half + 1, begun)
                            wait(pool, split_b, u * 2 + half + 1, begun)
                            pool.tensor_tensor(qk_part[2][:, cols], qk_rest[:, cols], qk_part[1][:, cols], ALU.subtract).then_inc(split_s, 1)
                        if t == RESID_AT:
                            if cur:
                                wait(pool, h2_s, w * 4, begun)
                                pool.tensor_tensor(resid[:, :, :], emb[:, :, :], b_o[:, :].unsqueeze(1).broadcast_to((P, NT, C)),
                                                   ALU.add).then_inc(resid_s, 1)
                            if nxt:
                                wait(pool, tok_in, (w + 1) * 16 + 16, begun)
                                wait(pool, resid_s, w + 1, begun)
                                wait(pool, xn_s, (w + 1) * NT, begun)
                                for n in range(NT):
                                    pool.indirect_dma_start(emb[:, n, :], None, dram["table"],
                                                            bass.IndirectOffsetOnAxis(ap=tok[:, n:n + 1], axis=0)).then_inc(emb_in, 16)
                        if t == EMB_AT and nxt and cur:
                            wait(pool, emb_in, (w + 2) * 16 * NT, begun)
                            pool.tensor_tensor(emb[:, :, :], emb[:, :, :], b_tok[:, :].unsqueeze(1).broadcast_to((P, NT, C)),
                                               ALU.add).then_inc(emb_b, 1)
                        if t == LN1_AT and nxt:
                            wait(pool, x_turn, (w + 1) * 4, begun)
                            layer_norm(emb, mv1, var1_sb[:, :], rstd1, xn, stats1, var1, rstd1_s, xn_s, w + 1, cur)
                        if t == LN2_AT and prv:
                            wait(pool, x2_turn, (w - 1) * 4, begun)
                            wait(pool, sent, (w - 1) * 16 * 2 * NT, begun)
                            layer_norm(h2, mv2, var2_sb[:, :], rstd2, xn2, stats2, var2, rstd2_s, xn2_s, w - 1, cur)
                        if t in SEND_AT and prv:
                            k = SEND_AT.index(t)
                            if k == 0:
                                wait(pool, slots_s, w * 3, begun)
                                pool.wait_ge(zeroed, 16 * (G * SB + 1))
                            else:
                                wait(pool, second_s, w, begun)
                            for n in range(NT):
                                pool.indirect_dma_start(dram["slots"], bass.IndirectOffsetOnAxis(ap=slot_at[:, n, k:k + 1], axis=0),
                                                        xn2[:, n, :], None, bounds_check=SLOTS - 1, oob_is_err=False).then_inc(sent, 16)

                pool.wait_ge(consts, CONSTS)
                windows(pool, window)
                pool.wait_ge(zeroed, 16 * (G * SB + 1))
                wait(pool, sent, NB * 16 * 2 * NT, begun)


            @block.scalar
            def _(act):
                def window(w, flags):
                    prv, cur, nxt = flags
                    for t in range(WIN):
                        g, o = t // STEPS, t % STEPS
                        for at, lu, nh in ((O_AT[0], g, 0), (O_AT[1], g - 1, 1)):
                            if o == at and here(flags, lu):
                                u = w * G + lu
                                act.wait_ge(av_s, u * NT * 2 + nh * NT + NT)
                                wait(act, o_turn, (u - 1) * 2 + nh + 1)
                                act.activation(oT[:, nh, :], o_ps[:, :], ACT.Copy).then_inc(oT_s, 1)
                        if cur:
                            hp = t % 2
                            if hp == 0:
                                wait(act, av_s, w * (WIN // 2) + t // 2 - 1)
                            for i in range(2):
                                act.wait_ge(s2_s, (w * WIN + t) * 2 + i + 1)
                                act.activation(probs[(t // 2) % 2][:, 2 * hp + i, :], s2_ps[:, RING[2 * o + i], :], ACT.Exp,
                                               scale=HD ** -0.5).then_inc(exp_s, 1)
                        work = small_work(t - 1)
                        if work is None or not here(flags, work[1]):
                            continue
                        name, lu, part = work
                        u, b, gb = w * G + lu, w + lu // G, lu % G
                        b_before, g_before = w + (lu - 1) // G, (lu - 1) % G
                        if name == "qk":
                            cols = slice(512 * part, 512 * part + 512)
                            act.wait_ge(qk_s, u * 2 + part + 1)
                            wait(act, split_s, (u - 1) * 2 + part + 1)
                            act.activation(qk_full[:, cols], m_ps[:, :], ACT.Identity, bias=b_qk[:, gb:gb + 1]).then_inc(qk_fulls, 1)
                            wait(act, stack_in[g_before], (b_before + 1) * 192)
                            act.activation(qk_part[0][:, cols], m_ps[:, :], ACT.Identity, bias=b_qk[:, gb:gb + 1]).then_inc(qk_out, 1)
                        elif name == "max_turn":
                            act.wait_ge(max_turn, u + 1)
                            wait(act, max_in[g_before], (b_before + 1) * 16)
                            act.activation(max_rows[:, :], m_bf[0:3 * HG * NT, 0:P], ACT.Copy).then_inc(max_rows_s, 1)
                        elif name in ("x_turn", "on_turn", "x2_turn"):
                            came, went, dst, free, n = {
                                "x_turn": (x_turn, xT_s, xnT, v_turn, b * G),
                                "on_turn": (on_turn, onT_s, turned, gate_mm, b),
                                "x2_turn": (x2_turn, x2T_s, turned, out_mm, b * 4 + 4),
                            }[name]
                            act.wait_ge(came, b * 4 + part + 1)
                            wait(act, free, n)
                            act.activation(dst[:, :, 2 * P * part:2 * P * part + 2 * P],
                                           m_ps[:, :].rearrange("p (c n) -> p c n", c=CC), ACT.Copy).then_inc(went, 1)
                        elif name == "gate":
                            act.wait_ge(gate_mm, b + 1)
                            wait(act, route, b * ROUTE1)
                            act.activation(gate_e[:, :, :].rearrange("p n e -> p (n e)"), m_ps[:, 0:NT * E_], ACT.Exp,
                                           scale=-1.0).then_inc(gate_s, 1)

                act.wait_ge(loads, 16 * LOADS)
                windows(act, window)

            @block.vector
            def _(dve):
                def then(ins, s, value):
                    ins.then_inc(s, 1)
                    dve.wait_ge(s, value)

                def statistics(src, stat, mv, stat_done, b, part):
                    for n in (2 * part, 2 * part + 1):
                        dve.bn_stats(stat[:, n, :], src[:, n, :]).then_inc(stat_done, 1)
                    wait(dve, stat_done, b * (2 * NT) + 4 * part + 2, begun)
                    for n in (2 * part, 2 * part + 1):
                        dve.bn_aggr(mv[:, n, :], stat[:, n, :]).then_inc(stat_done, 1)

                def normalise(src, mv, rstd, dst, rstd_done, out_done, b):
                    dve.wait_ge(rstd_done, b + 1)
                    for n in range(NT):
                        dve.tensor_scalar(dst[:, n, 0:C], src[:, n, :], mv[:, n, 0:1], rstd[:, n:n + 1],
                                          ALU.subtract, ALU.mult).then_inc(out_done, 1)

                def choose_experts(b, at):
                    k = b * ROUTE1
                    k2 = k + 2 + 2 * NT
                    if at == 0:
                        dve.wait_ge(gate_s, b + 1)
                        then(dve.tensor_scalar(gate_p[:, :, :], gate_e[:, :, :], 1.0, None, ALU.add), route, k + 1)
                        dve.reciprocal(gate_p[:, :, :], gate_p[:, :, :]).then_inc(route, 1)
                    elif at in (1, 2):
                        wait(dve, route, k + 2, begun)
                        for n in range(4 * at - 4, 4 * at):
                            dve.max(top8[:, n, :], gate_p[:, n, :]).then_inc(route, 1)
                    elif at in (3, 4):
                        wait(dve, route, k + 2 + NT, begun)
                        for n in range(4 * at - 12, 4 * at - 8):
                            dve.max_index(top8_at[:, n, :], top8[:, n, :], gate_p[:, n, :]).then_inc(route, 1)
                    elif at == 5:
                        dve.wait_ge(route, k2)
                        then(dve.tensor_tensor(gsum[:, :], top8[:, :, 0], top8[:, :, 1], ALU.add), route, k2 + 1)
                        dve.tensor_scalar(gsum[:, :], gsum[:, :], 1e-6, None, ALU.add).then_inc(route, 1)
                    elif at == 6:
                        dve.wait_ge(route, k2 + 2)
                        then(dve.reciprocal(gsum[:, :], gsum[:, :]), route, k2 + 3)
                        dve.tensor_tensor(weight2[:, :, :], top8[:, :, 0:2], gsum[:, :].unsqueeze(2).broadcast_to((P, NT, 2)),
                                          ALU.mult).then_inc(route, 1)
                        dve.tensor_copy(sel[:, :, :], top8_at[:, :, 0:2]).then_inc(route, 1)
                    elif at == 7:
                        dve.wait_ge(route, k2 + 5)
                        for i in range(2):
                            dve.tensor_tensor(hot[i][:, :, :], expert_iota[:, :].unsqueeze(1).broadcast_to((P, NT, E_)),
                                              sel[:, :, i:i + 1].broadcast_to((P, NT, E_)), ALU.is_equal).then_inc(route, 1)
                    elif at == 8:
                        dve.wait_ge(route, k2 + 7)
                        wait(dve, rank_mm, b)
                        dve.tensor_tensor(hot_bf[:, :, :], hot[0][:, :, :], hot[1][:, :, :], ALU.add).then_inc(route, 1)

                def give_slots(b, at):
                    k = b * ROUTE2
                    if at == 0:
                        dve.wait_ge(rank_mm, b + 1)
                        ranks = m_ps[:, 0:NT * E_].rearrange("p (n e) -> p n e", n=NT)
                        for i in range(2):
                            dve.tensor_tensor(picked[i][:, :, :], ranks, hot[i][:, :, :], ALU.mult).then_inc(picked_s, 1)
                    elif at == 1:
                        dve.wait_ge(picked_s, b * 2 + 2)
                        for i in range(2):
                            dve.tensor_reduce(rank[:, :, i], picked[i][:, :, :], AX.X, ALU.add).then_inc(route2, 1)
                        dve.tensor_reduce(hot_sum[:, :], hot_bf[:, :, :].rearrange("p n e -> p e n"), AX.X, ALU.add).then_inc(route2, 1)
                    elif at == 2:
                        dve.wait_ge(route2, k + 3)
                        dve.tensor_tensor(carry_bf[:, :], carry_bf[:, :], hot_sum[:, :], ALU.add).then_inc(route2, 1)
                        dve.tensor_scalar(valid[:, :, :], rank[:, :, :], float(CAP), None, ALU.is_lt).then_inc(route2, 1)
                        dve.scalar_tensor_tensor(slot[:, :, :], sel[:, :, :], float(CAP), rank[:, :, :], ALU.mult, ALU.add).then_inc(route2, 1)
                    elif at == 3:
                        dve.wait_ge(route2, k + 6)
                        then(dve.scalar_tensor_tensor(slot[:, :, :], slot[:, :, :], float(SLOTS), valid[:, :, :], ALU.subtract, ALU.mult), route2, k + 7)
                        wait(dve, sent, b * 16 * 2 * NT)
                        dve.tensor_scalar(slot_at[:, :, :], slot[:, :, :], float(SLOTS), None, ALU.add).then_inc(slots_s, 1)
                        dve.tensor_copy(xn2[:, :, C], token[:, :]).then_inc(slots_s, 1)
                        dve.tensor_copy(xn2[:, :, C + 1], weight2[:, :, 0]).then_inc(slots_s, 1)
                    elif at == 4:
                        dve.wait_ge(slots_s, b * 3 + 3)
                        dve.tensor_scalar(token[:, :], token[:, :], float(N), None, ALU.add).then_inc(route2, 1)
                        dve.wait_ge(route2, k + 8)

                def window(w, flags):
                    prv, cur, nxt = flags
                    for t in range(WIN):
                        g, o = t // STEPS, t % STEPS
                        ahead = t + LEAD
                        lu, step = ahead // STEPS, ahead % STEPS
                        if here(flags, lu):
                            u = w * G + lu
                            if step == 0:
                                wait(dve, neg_s, (u - 1) * 5 + 1)
                            for half in range(2):
                                dve.wait_ge(s1_s, u * 64 + step * 2 + half + 1)
                                dve.tensor_reduce(half_max[:, step, half:half + 1], s1_ps[:, RING[2 * step + half], :], AX.X, ALU.max).then_inc(s1_max, 1)
                            if step == STEPS - 1:
                                k = u * 5
                                dve.wait_ge(s1_max, u * 64 + 64)
                                then(dve.tensor_reduce(neg_max[:, :], half_max[:, :, :], AX.X, ALU.max, negate=True), neg_s, k + 1)
                                wait(dve, max_turn, u)
                                then(dve.tensor_copy(neg_part[:, 0, :], neg_max[:, :]), neg_s, k + 2)
                                then(dve.tensor_tensor(neg_rest[:, :], neg_max[:, :], neg_part[:, 0, :], ALU.subtract), neg_s, k + 3)
                                then(dve.tensor_copy(neg_part[:, 1, :], neg_rest[:, :]), neg_s, k + 4)
                                dve.tensor_tensor(neg_part[:, 2, :], neg_rest[:, :], neg_part[:, 1, :], ALU.subtract).then_inc(neg_s, 1)
                        if t - 2 in OP_AT and prv:
                            part = OP_AT.index(t - 2)
                            dve.wait_ge(h2_s, (w - 1) * 4 + part + 1)
                            if part == 0:
                                wait(dve, xn2_s, (w - 1) * NT)
                            statistics(h2, stat2, mv2, stats2, w - 1, part)
                        if t == EMB_AT and nxt and not cur:
                            dve.wait_ge(emb_in, (w + 2) * 16 * NT)
                            dve.tensor_tensor(emb[:, :, :], emb[:, :, :], b_tok[:, :].unsqueeze(1).broadcast_to((P, NT, C)),
                                              ALU.add).then_inc(emb_b, 1)
                        if t in STAT1_AT and nxt:
                            dve.wait_ge(emb_b, w + 2)
                            if t == STAT1_AT[0]:
                                wait(dve, xn_s, (w + 1) * NT)
                            statistics(emb, stat1, mv1, stats1, w + 1, STAT1_AT.index(t))
                        if not cur and nxt and t == LN1_AT:
                            normalise(emb, mv1, rstd1, xn, rstd1_s, xn_s, w + 1)
                        if not cur and prv and t == LN2_AT:
                            dve.wait_ge(x2_turn, (w - 1) * 4)
                            dve.wait_ge(sent, (w - 1) * (16 * 2 * NT))
                            normalise(h2, mv2, rstd2, xn2, rstd2_s, xn2_s, w - 1)
                        if GATE_AT + 1 < t <= GATE_AT + 10 and prv:
                            choose_experts(w - 1, t - GATE_AT - 2)
                        if RANK_AT + 1 < t <= RANK_AT + 5 and prv:
                            give_slots(w - 1, t - RANK_AT - 1)
                        if t == SEND_AT[1] - 2 and prv:
                            dve.wait_ge(sent, (w * 2 - 1) * (16 * NT))
                            dve.tensor_copy(xn2[:, :, C + 1], weight2[:, :, 1]).then_inc(second_s, 1)
                        work = small_work(t - 1)
                        if work is None or not here(flags, work[1]):
                            continue
                        name, lu, part = work
                        u, b, gb = w * G + lu, w + lu // G, lu % G
                        if name == "o_turn":
                            dve.wait_ge(o_turn, u * 2 + part + 1)
                            heads = m_ps[:, :].rearrange("p (n h d) -> p n h d", n=4, h=HG)
                            sums = rsum[:, part, :].rearrange("p (n h) -> p n h", n=4)
                            then(dve.reciprocal(sums, heads[:, :, :, HD]), rsum_s, u * 2 + part + 1)
                            if gb == 0:
                                wait(dve, on_turn, b * 4)
                            dst = o_n[:, 4 * part:4 * part + 4, 64 * gb:64 * gb + 64].rearrange("p n (h d) -> p n h d", h=HG)
                            dve.tensor_tensor(dst, heads[:, :, :, 0:HD], sums.unsqueeze(3).broadcast_to((P, 4, HG, HD)), ALU.mult).then_inc(on_s, 1)
                        elif name == "v":
                            dve.wait_ge(v_turn, u + part + 1)
                            wait(dve, av_s, (u + 2 - G) * 2 * NT)
                            for i in range(2):
                                src = m_ps[:, :].rearrange("p (n g h d) -> p g n h d", n=4, g=2, h=HG)[:, i]
                                bias = b_v[:, 64 * (gb + i):64 * (gb + i) + 64].rearrange("p (h d) -> p h d", h=HG)
                                dve.tensor_tensor(v_sb[gb + i][:, 4 * part:4 * part + 4, :, 0:HD], src,
                                                  bias.unsqueeze(1).broadcast_to((P, 4, HG, HD)), ALU.add).then_inc(v_s, 1)
                        elif name == "out":
                            dve.wait_ge(out_mm, b * 4 + part + 1)
                            dve.wait_ge(resid_s, b + 1)
                            if part == 0:
                                wait(dve, h2_st, b * 16)
                                wait(dve, xn2_s, b * NT)
                            dve.tensor_tensor(h2[:, 2 * part:2 * part + 2, :], m_ps[:, :].rearrange("p (n c) -> p n c", n=2),
                                              resid[:, 2 * part:2 * part + 2, :], ALU.add).then_inc(h2_s, 1)
                        elif name == "rank":
                            give_slots(b, 0)

                for g in range(G):
                    dve.memset(k_stack[g][KQ:KS, :], 1.0).then_inc(ones_s, 1)
                dve.wait_ge(consts, CONSTS)
                dve.wait_ge(loads, 16 * LOADS)
                windows(dve, window)

            @block.tensor
            def _(pe):
                def turn4(src, part, done):
                    for c in range(CC):
                        for n in range(2):
                            last = pe.transpose(m_ps[:, (2 * c + n) * P:(2 * c + n + 1) * P],
                                                src[:, 2 * part + n, c * P:(c + 1) * P], ident[:, :])
                    last.then_inc(done, 1)

                def do_small(work, w):
                    name, lu, part = work
                    u, b, gb = w * G + lu, w + lu // G, lu % G
                    if name == "o_turn":
                        pe.wait_ge(oT_s, u * 2 + part + 1)
                        for n in range(4):
                            last = pe.transpose(m_ps[:, n * P:(n + 1) * P], oT[:, part, n * P:(n + 1) * P], ident[:, :])
                        last.then_inc(o_turn, 1)
                    elif name == "qk":
                        if part == 0:
                            pe.wait_ge(xT_s, b * 4 + 4)
                        for c in range(CC):
                            last = pe.matmul(m_ps[:, :], wqk[:, c, gb, :], xnT[:, c, 512 * part:512 * part + 512],
                                             start=(c == 0), stop=(c == CC - 1))
                        last.then_inc(qk_s, 1)
                    elif name == "v":
                        for n in range(4):
                            at = P * (4 * part + n)
                            for c in range(CC):
                                last = pe.matmul(m_ps[:, P * n:P * n + P], xnT[:, c, at:at + P], wv[:, c, 64 * gb:64 * gb + P],
                                                 start=(c == 0), stop=(c == CC - 1))
                        last.then_inc(v_turn, 1)
                    elif name == "max_turn":
                        pe.wait_ge(neg_s, u * 5 + 5)
                        pe.transpose(m_bf[0:3 * HG * NT, 0:P], neg_part[:, :, :].rearrange("p a n -> p (a n)"), ident_bf[:, :]).then_inc(max_turn, 1)
                    elif name == "on_turn":
                        pe.wait_ge(on_s, b * G * 2 + G * 2)
                        turn4(o_n, part, on_turn)
                    elif name == "x_turn":
                        pe.wait_ge(xn_s, b * NT + 2 * part + 2)
                        turn4(xn, part, x_turn)
                    elif name == "x2_turn":
                        pe.wait_ge(xn2_s, b * NT + 2 * part + 2)
                        turn4(xn2, part, x2_turn)
                    elif name == "out":
                        pe.wait_ge(onT_s, b * 4 + part + 1)
                        for n in range(2):
                            at = (2 * part + n) * P
                            for c in range(CC):
                                last = pe.matmul(m_ps[:, C * n:C * n + C], turned[:, c, at:at + P], wo[:, c, :],
                                                 start=(c == 0), stop=(c == CC - 1))
                        last.then_inc(out_mm, 1)
                    elif name == "gate":
                        pe.wait_ge(x2T_s, b * 4 + 4)
                        for n in range(NT):
                            for c in range(CC):
                                last = pe.matmul(m_ps[:, E_ * n:E_ * n + E_], turned[:, c, P * n:P * n + P], gw[:, c, :],
                                                 start=(c == 0), stop=(c == CC - 1))
                        last.then_inc(gate_mm, 1)
                    elif name == "rank":
                        pe.wait_ge(route, b * ROUTE1 + ROUTE1)
                        wait(pe, route2, b * ROUTE2)
                        flat = hot_bf[:, :, :].rearrange("p n e -> p (n e)")
                        pe.matmul(m_ps[:, 0:NT * E_], before_bf[:, :], flat, start=True, stop=False)
                        for n in range(1, NT):
                            pe.matmul(m_ps[:, n * E_:NT * E_], ones_bf[:, :], flat[:, 0:(NT - n) * E_], start=False, stop=False)
                        pe.matmul(m_ps[:, 0:NT * E_], ones_bf[:, :], carry_bf[:, :].unsqueeze(1).broadcast_to((P, NT, E_)),
                                  start=False, stop=True).then_inc(rank_mm, 1)

                def window(w, flags):
                    prv, cur, nxt = flags
                    before = ("max_turn", 0, 0) if cur else ("o_turn", -1, 0) if prv else None
                    for t in range(WIN):
                        ahead = t + LEAD
                        lu, step = ahead // STEPS, ahead % STEPS
                        g, o = t // STEPS, t % STEPS
                        nh, mt, hp = o // 16, (o % 16) // 2, o % 2
                        if here(flags, lu) and step == 0:
                            pe.wait_ge(stack_in[lu % G], (w + lu // G + 1) * 192)
                        if cur and o == 0:
                            pe.wait_ge(max_in[g], (w + 1) * 16)
                        for i in range(2):
                            if here(flags, lu):
                                u, gb = w * G + lu, lu % G
                                hh, n = step // NT, step % NT
                                wait(pe, s1_max, (w + 3) * (G * SC) + ((lu - 3 * G) * SC + bank_user_before(2 * step + i) + 1))
                                pe.matmul(s1_ps[:, RING[2 * step + i], :], q_stack[gb][0:KQ, hh * N + n * P:hh * N + n * P + P],
                                          k_stack[gb][0:KQ, hh * N + i * 512:hh * N + i * 512 + 512],
                                          start=True, stop=True).then_inc(s1_s, 1)
                            if cur:
                                hh = 2 * hp + i
                                wait(pe, exp_s, (w * G + g) * SC + bank_user_before(2 * o + i) + 1)
                                pe.matmul(s2_ps[:, RING[2 * o + i], :], k_stack[g][0:KS, hh * N + mt * P:hh * N + mt * P + P],
                                          q_stack[g][0:KS, hh * N + nh * 512:hh * N + nh * 512 + 512],
                                          start=True, stop=True).then_inc(s2_s, 1)
                        lp = (t - 1) // 2 - 1
                        if t % 2 == 1 and (cur if lp >= 0 else prv):
                            q = w * (WIN // 2) + lp
                            g, mt = (lp // 16) % G, lp % NT
                            pe.wait_ge(exp_s, q * 4 + 4)
                            if lp % 16 == 0:
                                pe.wait_ge(v_s, (w * G + g // 2 * 2 + 2) * 2)
                            if mt == 0:
                                wait(pe, oT_s, w * (2 * G) + lp // NT)
                            for hh in range(HG):
                                last = pe.matmul(o_ps[32 * hh:32 * hh + 32, :], v_sb[g][:, mt, hh, :], probs[lp % 2][:, hh, :],
                                                 start=(mt == 0), stop=(mt == NT - 1))
                            last.then_inc(av_s, 1)
                        work = small_work(t)
                        if work is not None and here(flags, work[1]):
                            if before is not None:
                                wait(pe, *taken(before, w))
                            do_small(work, w)
                            before = work

                pe.wait_ge(consts, CONSTS)
                pe.wait_ge(ones_s, G)
                pe.wait_ge(loads, 16 * LOADS)
                windows(pe, window)


def experts(nc, begun, dram, CAP):
    ST = CAP // TE
    SB = ST // P
    YB = (SB + 1) // 2
    PAIRS = E_ // 2
    NI = E_ * TE
    HI, LO = 0, 1
    PARTS = ((HI, HI), (HI, LO), (LO, HI))
    assert ST * TE == CAP and SB * P == ST and ST <= 512
    ctx = ExitStack()
    with ctx:
        def sb(name, shape, dt=F32):
            return ctx.enter_context(nc.sbuf_tensor(name, shape, dt))

        def sem(name):
            return ctx.enter_context(nc.semaphore(name))

        ident = sb("x_ident", [P, P])
        w1_raw = sb("w1_raw", [P, CC, F])
        w2_raw = sb("w2_raw", [P, FC, C])
        w1 = [[sb(f"w1_{e}_{h}", [P, CC, F], F32R) for h in range(2)] for e in range(2)]
        w2 = [[sb(f"w2_{e}_{h}", [P, FC, C], F32R) for h in range(2)] for e in range(2)]
        rows = [sb(f"rows{i}", [P, SB, ROW]) for i in range(2)]
        token_of = sb("token_of", [P, TE, SB], I32)
        weight_of = sb("weight_of", [P, TE, SB])
        rowsT = [[sb(f"rowsT{i}_{h}", [P, CC, ST], F32R) for h in range(2)] for i in range(2)]
        hid_full = [sb(f"hid_full{i}", [P, FC, ST]) for i in range(2)]
        hid = [[sb(f"hid{i}_{h}", [P, FC, ST], F32R) for h in range(2)] for i in range(2)]
        y = [sb(f"y{i}", [P, SB, C]) for i in range(2)]
        turn_ps = ctx.enter_context(nc.psum_tensor("turn_ps", [P, CC, 512], F32))
        hid_ps = ctx.enter_context(nc.psum_tensor("hid_ps", [P, FC, 512], F32))
        y_ps = ctx.enter_context(nc.psum_tensor("y_ps", [P, 2, 512], F32))

        mask = sem("x_mask")
        w_in = [sem(f"w_in{n}") for n in range(2)]
        w_hi = sem("w_hi")
        w_lo = sem("w_lo")
        rows_in = [sem(f"rows_in{i}") for i in range(2)]
        turn_mm = sem("turn_mm")
        rowsT_hi = sem("rowsT_hi")
        rowsT_lo = sem("rowsT_lo")
        hid_mm = sem("hid_mm")
        gelu_s = sem("gelu_s")
        hid_lo = sem("hid_lo")
        y_mm = sem("y_mm")
        y_s = sem("y_s")
        known = sem("known")
        added = sem("added")
        ADDS = 16 * SB

        def pairs(eng, body):
            body(0, True, False)
            with eng.Fori(1, PAIRS - 1) as j:
                body(j, False, False)
            body(PAIRS - 1, False, True)

        with nc.Block() as block:

            @block.gpsimd
            def _(pool):
                pool.memset(ident[:, :], 0.0).then_inc(mask, 1)
                pool.wait_ge(mask, 1)
                pool.affine_select(out=ident[:, :], in_=ident[:, :], compare_op=ALU.not_equal, fill=1.0, base=0,
                                   pattern=[[-1, P]], channel_multiplier=1).then_inc(mask, 1)

                def body(j, first, last):
                    for k in range(2 * TE):
                        i = j * (2 * TE) + k
                        wait(pool, known, i * 2 + 2, begun)
                        wait(pool, y_s, i * YB + YB, begun)
                        wait(pool, added, i * ADDS, begun)
                        for n in range(SB):
                            pool.indirect_dma_start(dram["out_rows"], bass.IndirectOffsetOnAxis(ap=token_of[:, k % TE, n:n + 1], axis=0),
                                                    y[k % 2][:, n, :], None, compute_op=ALU.add).then_inc(added, 16)

                pairs(pool, body)
                pool.wait_ge(added, NI * ADDS)

            @block.sync
            def _(sp):
                def load_rows(i, par):
                    sp.dma_start(rows[par][:, :, :], dram["slots_t"][i]).then_inc(rows_in[par], 16)

                def load_w(e):
                    sp.dma_start(w1_raw[:, :, :], dram["w1"][e]).then_inc(w_in[0], 16)
                    sp.dma_start(w2_raw[:, :, :], dram["w2"][e]).then_inc(w_in[1], 16)

                load_rows(0, 0)
                load_w(0)
                load_rows(1, 1)

                def body(j, first, last):
                    for k in range(2 * TE):
                        i = j * (2 * TE) + k
                        if not (last and k >= 2 * TE - 2):
                            wait(sp, turn_mm, i + 1, begun)
                            wait(sp, known, i * 2 + 2, begun)
                            load_rows(i + 2, k % 2)
                        if k % TE == 0 and not (last and k > 0):
                            wait(sp, w_lo, j * 4 + 2 * (k // TE) + 2, begun)
                            load_w(j * 2 + k // TE + 1)

                pairs(sp, body)

            @block.scalar
            def _(act):
                def turned_high(i, par):
                    act.wait_ge(turn_mm, i + 1)
                    wait(act, hid_mm, (i - 1) * FC)
                    act.activation(rowsT[par][HI][:, :, :], turn_ps[:, :, 0:ST], ACT.Copy).then_inc(rowsT_hi, 1)

                def body(j, first, last):
                    for k in range(2 * TE):
                        i = j * (2 * TE) + k
                        wait(act, y_mm, (i - 1) * YB)
                        for f in range(FC):
                            act.wait_ge(hid_mm, i * FC + f + 1)
                            act.activation(hid_full[k % 2][:, f, :], hid_ps[:, f, 0:ST], ACT.Gelu).then_inc(gelu_s, 1)
                            act.activation(hid[k % 2][HI][:, f, :], hid_ps[:, f, 0:ST], ACT.Gelu).then_inc(gelu_s, 1)
                        if not (last and k == 2 * TE - 1):
                            turned_high(i + 1, (k + 1) % 2)

                turned_high(0, 0)
                pairs(act, body)

            @block.vector
            def _(dve):
                def split_weights(e, par, which=(0, 1)):
                    wait(dve, y_mm, (e - 1) * TE * YB)
                    for n in which:
                        raw, w = (w1_raw, w2_raw)[n], (w1, w2)[n][par]
                        dve.wait_ge(w_in[n], e * 16 + 16)
                        dve.tensor_copy(w[HI][:, :, :], raw[:, :, :]).then_inc(w_hi, 1)
                        dve.wait_ge(w_hi, e * 2 + n + 1)
                        dve.tensor_tensor(w[LO][:, :, :], raw[:, :, :], w[HI][:, :, :].bitcast(F32), ALU.subtract).then_inc(w_lo, 1)

                def turned_low(i, par, of, nth):
                    dve.wait_ge(rowsT_hi, i + 1)
                    wait(dve, hid_mm, (i - 1) * FC)
                    dve.tensor_tensor(rowsT[par][LO][:, :, :], turn_ps[:, :, 0:ST], rowsT[par][HI][:, :, :].bitcast(F32),
                                      ALU.subtract).then_inc(rowsT_lo, 1)
                    dve.wait_ge(rows_in[par], nth * 16)
                    dve.tensor_copy(token_of[:, of, :], rows[par][:, :, C]).then_inc(known, 1)
                    dve.tensor_copy(weight_of[:, of, :], rows[par][:, :, C + 1]).then_inc(known, 1)

                def copy_out(i, par, of):
                    dve.wait_ge(known, i * 2 + 2)
                    wait(dve, added, (i - 1) * ADDS)
                    for q in range(YB):
                        n = min(2, SB - 2 * q)
                        dve.wait_ge(y_mm, i * YB + q + 1)
                        dve.tensor_tensor(y[par][:, 2 * q:2 * q + n, :], y_ps[:, q, 0:n * C].rearrange("p (n c) -> p n c", n=n),
                                          weight_of[:, of, 2 * q:2 * q + n].unsqueeze(2).broadcast_to((P, n, C)), ALU.mult).then_inc(y_s, 1)

                def body(j, first, last):
                    for k in range(2 * TE):
                        i = j * (2 * TE) + k
                        wait(dve, y_mm, (i - 1) * YB)
                        for f in range(FC):
                            dve.wait_ge(gelu_s, i * (2 * FC) + 2 * f + 2)
                            dve.tensor_tensor(hid[k % 2][LO][:, f, :], hid_full[k % 2][:, f, :], hid[k % 2][HI][:, f, :].bitcast(F32),
                                              ALU.subtract).then_inc(hid_lo, 1)
                        if not (last and k == 2 * TE - 1):
                            turned_low(i + 1, (k + 1) % 2, (k + 1) % TE, j * TE + (k + 1) // 2 + 1)
                        if not (first and k == 0):
                            copy_out(i - 1, (k - 1) % 2, (k - 1) % TE)
                        if k % TE == 2 and not (last and k > TE):
                            split_weights(j * 2 + k // TE + 1, (k // TE + 1) % 2)

                split_weights(0, 0, (0,))
                turned_low(0, 0, 0, 1)
                split_weights(0, 0, (1,))
                pairs(dve, body)
                copy_out(NI - 1, 1, TE - 1)

            @block.tensor
            def _(pe):
                def turn(i, par, nth):
                    pe.wait_ge(rows_in[par], nth * 16)
                    wait(pe, rowsT_lo, i)
                    for c in range(CC):
                        for n in range(SB):
                            last = pe.transpose(turn_ps[:, c, n * P:(n + 1) * P], rows[par][:, n, c * P:(c + 1) * P], ident[:, :])
                    last.then_inc(turn_mm, 1)

                def first_product(i, par, e_par):
                    pe.wait_ge(rowsT_lo, i + 1)
                    for f in range(FC):
                        wait(pe, gelu_s, (i - 1) * (2 * FC) + 2 * f + 2)
                        terms = [(c, a, b) for c in range(CC) for a, b in PARTS]
                        for c, a, b in terms:
                            last = pe.matmul(hid_ps[:, f, 0:ST], w1[e_par][a][:, c, f * P:(f + 1) * P], rowsT[par][b][:, c, :],
                                             start=((c, a, b) == terms[0]), stop=((c, a, b) == terms[-1]))
                        last.then_inc(hid_mm, 1)

                def second_product(i, par, e_par, w_parts):
                    pe.wait_ge(hid_lo, i * FC + FC)
                    pe.wait_ge(w_lo, w_parts)
                    for q in range(YB):
                        wait(pe, y_s, (i - 1) * YB + q + 1)
                        for n in range(2 * q, min(2 * q + 2, SB)):
                            terms = [(f, a, b) for f in range(FC) for a, b in PARTS]
                            for f, a, b in terms:
                                last = pe.matmul(y_ps[:, q, (n % 2) * C:(n % 2) * C + C], hid[par][a][:, f, n * P:(n + 1) * P],
                                                 w2[e_par][b][:, f, :], start=((f, a, b) == terms[0]), stop=((f, a, b) == terms[-1]))
                        last.then_inc(y_mm, 1)

                def body(j, first, last):
                    for k in range(2 * TE):
                        i = j * (2 * TE) + k
                        if k % TE == 0:
                            pe.wait_ge(w_lo, j * 4 + 2 * (k // TE) + 1)
                        first_product(i, k % 2, k // TE)
                        if not (last and k == 2 * TE - 1):
                            nth = j * TE + (k + 1) // 2 + 1
                            turn(i + 1, (k + 1) % 2, nth)
                        if not (first and k == 0):
                            second_product(i - 1, (k - 1) % 2, ((k - 1) // TE) % 2, j * 4 + 2 * ((k - 1) // TE) + 2)

                pe.wait_ge(mask, 2)
                turn(0, 0, 1)
                pairs(pe, body)
                second_product(NI - 1, 1, 1, 2 * E_)


def lm_tower(nc, a, NB):
    CAP = int(1.25 * NB * N * 2 / E_)
    SLOTS = E_ * CAP
    ST = CAP // TE
    out = a["out"]
    slots = nc.dram_tensor("slot_rows", (SLOTS, ROW), F32).ap()
    dram = {
        "table": a["table"], "tok": a["tok"],
        "wqk": a["wqk"], "wv": a["wv"], "wo": a["wo"], "gw": a["gate"],
        "b_qk": a["b_qk"], "b_v": a["b_v"], "b_o": a["b_o"], "b_tok": a["b_tok"],
        "w1": a["w1"].rearrange("e (c p) f -> e p c f", p=P), "w2": a["w2"].rearrange("e (c p) d -> e p c d", p=P),
        "slots": slots, "slots_t": slots.rearrange("(i n p) c -> i p n c", p=P, n=ST // P),
        "out_rows": out, "out": out[0:NB * N, :].rearrange("(b n p) c -> b p n c", p=P, n=NT),
        "spare": out[NB * N:NB * N + ST, :].rearrange("(n p) c -> p n c", p=P),
    }
    with ExitStack() as ctx:
        begun = ctx.enter_context(nc.semaphore("begun"))
        attention_and_routing(nc, begun, dram, NB, CAP)
        experts(nc, begun, dram, CAP)


def out_rows(nb):
    return nb * N + int(1.25 * nb * N * 2 / E_) // TE


def lay_out(x, L0_tok_weight, L0_tok_bias, L0_attn_w_qkv, L0_attn_b_qkv, L0_attn_w_out, L0_attn_b_out,
            L0_ffn_gate_w, L0_ffn_w1, L0_ffn_w2):
    import numpy as np

    arr = lambda v: np.ascontiguousarray(np.asarray(v))
    by_chunk = lambda w: arr(np.asarray(w).T.reshape(CC, P, -1).transpose(1, 0, 2))
    nb = x.shape[0]
    w, b = np.asarray(L0_attn_w_qkv), np.asarray(L0_attn_b_qkv)
    qk_rows = np.array([[s * C + (g * HG + h) * HD + d for s in range(2) for d in range(HD) for h in range(HG)] for g in range(G)])
    return {
        "tok": arr(np.asarray(x).reshape(nb, NT, P).transpose(0, 2, 1)),
        "table": arr(np.asarray(L0_tok_weight).T),
        "wqk": arr(w[qk_rows.reshape(-1)].T.reshape(CC, P, G, P).transpose(1, 0, 2, 3)),
        "wv": by_chunk(w[2 * C:3 * C]), "wo": by_chunk(L0_attn_w_out), "gate": by_chunk(L0_ffn_gate_w),
        "b_qk": arr(b[qk_rows].T), "b_v": arr(b[2 * C:3 * C]), "b_o": arr(L0_attn_b_out), "b_tok": arr(L0_tok_bias),
        "w1": arr(L0_ffn_w1), "w2": arr(L0_ffn_w2),
    }


def kernel(**inputs):
    import numpy as np
    import concourse.bacc as bacc
    from concourse.bass_utils import run_bass_kernel_spmd

    nb = inputs["x"].shape[0]
    arrays = lay_out(**inputs)
    nc = bacc.Bacc("TRN2", target_bir_lowering=False, num_devices=1)
    a = {name: nc.dram_tensor("in_" + name, v.shape, mybir.dt.from_np(v.dtype), kind="ExternalInput").ap() for name, v in arrays.items()}
    a["out"] = nc.dram_tensor("out_rows", (out_rows(nb), C), F32, kind="ExternalOutput").ap()
    lm_tower(nc, a, nb)
    r = run_bass_kernel_spmd(nc, [{"in_" + name: v for name, v in arrays.items()}], core_ids=[0])
    return np.asarray(r.results[0]["out_rows"])[:nb * N].reshape(nb, N, C)
```
